# Optimizing a Trainium2 kernel written in Bass

```python
import numpy as np
import jax
import jax.numpy as jnp

def _softmax(x, axis=-1):
    return jax.nn.softmax(x, axis=axis)

def _gelu(x):
    return jax.nn.gelu(x, approximate=True)

def _silu(x):
    return jax.nn.silu(x)

def _sigmoid(x):
    return jax.nn.sigmoid(x)

def _layernorm(x, axis=-1, eps=1e-05):
    m = jnp.mean(x, axis=axis, keepdims=True)
    v = jnp.var(x, axis=axis, keepdims=True)
    return (x - m) / jnp.sqrt(v + eps)

def _scatter_add(tgt, idx, src, axis=0):
    return tgt.at[idx].add(src)

def _segment_sum(src, seg, n):
    return jax.ops.segment_sum(src, seg, n)
kernel_name = 'mk_vit_tower_d1_tok_img768_r4_dd4955'

def setup_inputs(seed: int=0):
    np.random.seed(seed)
    _w = jnp.asarray

    def _rec_inputs():
        import jax
        import jax.numpy as jnp
        _rk = jax.random.key(seed)
        x = -9.30917e-05 + 1.0002 * jax.random.normal(jax.random.fold_in(_rk, 1), (64, 3, 112, 112), jnp.float32)
        return x
    x = _rec_inputs()

    def _L0_tok_setup():
        import jax, jax.numpy as jnp
        import numpy as np
        PATCH = 16
        EPS = 1e-05

        def _shift(x, pad_spec):
            l, r, t, b = pad_spec
            H, W = (x.shape[2], x.shape[3])
            xp = jnp.pad(x, ((0, 0), (0, 0), (max(t, 0), max(b, 0)), (max(l, 0), max(r, 0))))
            h0 = -t if t < 0 else 0
            w0 = -l if l < 0 else 0
            return xp[:, :, h0:h0 + H, w0:w0 + W]
        key = jax.random.key(seed)
        k1, k2 = jax.random.split(key)
        B, C, H, Wd = (32, 3, 224, 224)
        patch_dim = PATCH * PATCH * 5 * C
        dim = 192
        x = jax.random.normal(k1, (B, C, H, Wd), dtype=jnp.float32)
        ln_gamma = jnp.ones((patch_dim,), dtype=jnp.float32)
        ln_beta = jnp.zeros((patch_dim,), dtype=jnp.float32)
        W = jax.random.normal(k2, (patch_dim, dim), dtype=jnp.float32) * patch_dim ** (-0.5)
        b = jnp.zeros((dim,), dtype=jnp.float32)
        return {'x': x, 'ln_gamma': ln_gamma, 'ln_beta': ln_beta, 'W': W, 'b': b}
    _L0_tok_all = _L0_tok_setup()
    _L0_tok_in = {k: v for k, v in _L0_tok_all.items() if k in ('ln_gamma', 'ln_beta', 'W', 'b')}
    del _L0_tok_all

    def _L0_attn_setup():
        import jax, jax.numpy as jnp
        import numpy as np
        N_HEAD = 12
        key = jax.random.key(seed)
        k1, k2, k3 = jax.random.split(key, 3)
        nx = 192
        B, S = (2, 512)
        return {'hidden_states': jax.random.normal(k1, (B, S, nx), dtype=jnp.float32), 'w_attn': jax.random.normal(k2, (nx, 3 * nx), dtype=jnp.float32) * 0.02, 'b_attn': jnp.zeros((3 * nx,), dtype=jnp.float32), 'w_proj': jax.random.normal(k3, (nx, nx), dtype=jnp.float32) * 0.02, 'b_proj': jnp.zeros((nx,), dtype=jnp.float32)}
    _L0_attn_all = _L0_attn_setup()
    _L0_attn_in = {k: v for k, v in _L0_attn_all.items() if k in ('w_attn', 'b_attn', 'w_proj', 'b_proj')}
    del _L0_attn_all

    def _L0_ffn_setup():
        import jax, jax.numpy as jnp
        import numpy as np
        B, S, D, F, E = (4, 512, 192, 768, 8)
        key = jax.random.key(seed)
        ks = jax.random.split(key, 5)
        return {'x': jax.random.normal(ks[0], (B, S, D), dtype=jnp.float32), 'Ws': jax.random.normal(ks[1], (D, E), dtype=jnp.float32) * 0.02, 'bs': jnp.zeros((E,), dtype=jnp.float32), 'W1': jax.random.normal(ks[2], (E, D, F), dtype=jnp.float32) * 0.02, 'b1': jnp.zeros((E, F), dtype=jnp.float32), 'W2': jax.random.normal(ks[3], (E, F, D), dtype=jnp.float32) * 0.02, 'b2': jnp.zeros((E, D), dtype=jnp.float32)}
    _L0_ffn_all = _L0_ffn_setup()
    _L0_ffn_in = {k: v for k, v in _L0_ffn_all.items() if k in ('Ws', 'bs', 'W1', 'b1', 'W2', 'b2')}
    del _L0_ffn_all
    return {'x': x, 'L0_tok_ln_gamma': _L0_tok_in['ln_gamma'], 'L0_tok_ln_beta': _L0_tok_in['ln_beta'], 'L0_tok_W': _L0_tok_in['W'], 'L0_tok_b': _L0_tok_in['b'], 'L0_attn_w_attn': _L0_attn_in['w_attn'], 'L0_attn_b_attn': _L0_attn_in['b_attn'], 'L0_attn_w_proj': _L0_attn_in['w_proj'], 'L0_attn_b_proj': _L0_attn_in['b_proj'], 'L0_ffn_Ws': _L0_ffn_in['Ws'], 'L0_ffn_bs': _L0_ffn_in['bs'], 'L0_ffn_W1': _L0_ffn_in['W1'], 'L0_ffn_b1': _L0_ffn_in['b1'], 'L0_ffn_W2': _L0_ffn_in['W2'], 'L0_ffn_b2': _L0_ffn_in['b2']}

def reference(x, L0_tok_ln_gamma, L0_tok_ln_beta, L0_tok_W, L0_tok_b, L0_attn_w_attn, L0_attn_b_attn, L0_attn_w_proj, L0_attn_b_proj, L0_ffn_Ws, L0_ffn_bs, L0_ffn_W1, L0_ffn_b1, L0_ffn_W2, L0_ffn_b2):
    import jax
    import jax.numpy as jnp

    def _L0_tok_ref(x, ln_gamma, ln_beta, W, b):
        import jax, jax.numpy as jnp
        import numpy as np
        PATCH = 16
        EPS = 1e-05

        def _shift(x, pad_spec):
            l, r, t, b = pad_spec
            H, W = (x.shape[2], x.shape[3])
            xp = jnp.pad(x, ((0, 0), (0, 0), (max(t, 0), max(b, 0)), (max(l, 0), max(r, 0))))
            h0 = -t if t < 0 else 0
            w0 = -l if l < 0 else 0
            return xp[:, :, h0:h0 + H, w0:w0 + W]
        shifts = [(1, -1, 0, 0), (-1, 1, 0, 0), (0, 0, 1, -1), (0, 0, -1, 1)]
        xs = jnp.concatenate([x] + [_shift(x, s) for s in shifts], axis=1)
        B, C5, H, Wd = xs.shape
        h, w = (H // PATCH, Wd // PATCH)
        t = xs.reshape(B, C5, h, PATCH, w, PATCH)
        t = t.transpose(0, 2, 4, 3, 5, 1)
        t = t.reshape(B, h * w, PATCH * PATCH * C5)
        mu = jnp.mean(t, axis=-1, keepdims=True)
        var = jnp.var(t, axis=-1, keepdims=True)
        tn = (t - mu) * jax.lax.rsqrt(var + EPS) * ln_gamma + ln_beta
        return jnp.einsum('bnp,pd->bnd', tn, W) + b

    def _L0_attn_ref(hidden_states, w_attn, b_attn, w_proj, b_proj):
        import jax, jax.numpy as jnp
        import numpy as np
        N_HEAD = 12
        B, S, nx = hidden_states.shape
        d_head = nx // N_HEAD
        qkv = hidden_states @ w_attn + b_attn
        q, k, v = jnp.split(qkv, 3, axis=-1)

        def split(x):
            return x.reshape(B, S, N_HEAD, d_head).transpose(0, 2, 1, 3)
        q, k, v = (split(q), split(k), split(v))
        w = jnp.einsum('bhsd,bhtd->bhst', q, k) / jnp.sqrt(jnp.float32(d_head))
        w = jax.nn.softmax(w, axis=-1)
        a = jnp.einsum('bhst,bhtd->bhsd', w, v)
        a = a.transpose(0, 2, 1, 3).reshape(B, S, nx)
        return a @ w_proj + b_proj

    def _L0_ffn_ref(x, Ws, bs, W1, b1, W2, b2):
        import jax, jax.numpy as jnp
        import numpy as np
        B, S, D, F, E = (4, 512, 192, 768, 8)
        b, s, d = x.shape
        xt = x.reshape(-1, d)
        logits = xt @ Ws + bs
        probs = jax.nn.softmax(logits, axis=-1)
        routes = jnp.argmax(probs, axis=-1)
        prob_max = jnp.max(probs, axis=-1)
        h = jax.nn.gelu(jnp.einsum('td,edf->etf', xt, W1) + b1[:, None, :], approximate=False)
        y = jnp.einsum('etf,efd->etd', h, W2) + b2[:, None, :]
        out = jnp.take_along_axis(y, routes[None, :, None], axis=0)[0]
        out = out * prob_max[:, None]
        return out.reshape(b, s, d)
    h = _L0_tok_ref(x, L0_tok_ln_gamma, L0_tok_ln_beta, L0_tok_W, L0_tok_b)
    h = h + _L0_attn_ref(_layernorm(h, axis=-1), L0_attn_w_attn, L0_attn_b_attn, L0_attn_w_proj, L0_attn_b_proj)
    h = h + _L0_ffn_ref(_layernorm(h, axis=-1), L0_ffn_Ws, L0_ffn_bs, L0_ffn_W1, L0_ffn_b1, L0_ffn_W2, L0_ffn_b2)
    return h

_drawn_inputs = setup_inputs


def setup_inputs(seed=0):
    import zlib

    import numpy as np

    out = dict(_drawn_inputs(seed))
    spreads = {'L0_tok_ln_gamma': (1.0, 0.2),
     'L0_tok_ln_beta': (0.0, 0.1),
     'L0_tok_b': (0.0, 0.1),
     'L0_attn_b_attn': (0.0, 0.279),
     'L0_attn_b_proj': (0.0, 0.1),
     'L0_ffn_bs': (0.0, 0.581),
     'L0_ffn_b1': (0.0, 0.8),
     'L0_ffn_b2': (0.0, 0.442)}
    factors = {'L0_attn_w_attn': 4.23, 'L0_ffn_W1': 3.879, 'L0_ffn_W2': 3.602}
    for name, (base, spread) in spreads.items():
        noise = np.random.default_rng([zlib.crc32(name.encode()), seed]).standard_normal(out[name].shape)
        drawn = base * np.exp(spread * noise) if base else spread * noise
        out[name] = jnp.asarray(drawn.astype(out[name].dtype))
    for name, factor in factors.items():
        out[name] = (out[name] * factor).astype(out[name].dtype)
    return out
```

```python
from collections import namedtuple
from contextlib import ExitStack

import concourse.bass as bass
from concourse import mybir
from concourse.alu_op_type import AluOpType as ALU

F32 = mybir.dt.float32
BF16 = mybir.dt.bfloat16
I32 = mybir.dt.int32
U32 = mybir.dt.uint32
ACT = mybir.ActivationFunctionType
AX = mybir.AxisListType.X

IMAGES, CH, SIDE, PATCH = 64, 3, 112, 16
GRID = SIDE // PATCH
SEQ = GRID * GRID
TOKENS = IMAGES * SEQ
DIM = 192
HALF = DIM // 2
HEADS, DH = 12, 16
GROUPS, HG = 2, 6
EXPERTS, FFN = 8, 768
SHIFTS = 5
PATCH_DIM = PATCH * PATCH * SHIFTS * CH
LN_EPS = 1e-5

PAIRS = IMAGES // 2
SLOT = 64
PAIR_TOKENS = 2 * SEQ
SPAN = SEQ + SLOT

CHUNKS = 8
MULTIPLICITIES = (5, 4, 3, 1)

TILE = 128
TILES = (TOKENS + EXPERTS * (TILE - 1)) // TILE
FT = FFN // 128
FH = FT // 2
ROW = 2 * DIM
VALUES = 5
SKIP = 8192

Step = namedtuple("Step", "n half par quad ring")


def window():
    pixels = []
    for r in range(-1, PATCH + 1):
        for q in range(-1, PATCH + 1):
            if 0 <= r < PATCH or 0 <= q < PATCH:
                m = sum(0 <= r + dr < PATCH and 0 <= q + dq < PATCH
                        for dr, dq in ((0, 0), (0, 1), (0, -1), (1, 0), (-1, 0)))
                pixels += [(m, r, q, c) for c in range(CH)]
    place, multiplicity, base = {}, [], 0
    for m in MULTIPLICITIES:
        mine = [x[1:] for x in pixels if x[0] == m]
        for n, x in enumerate(mine):
            place[x] = (n % CHUNKS, base + n // CHUNKS)
        rows = -(-len(mine) // CHUNKS)
        multiplicity += [m] * rows
        base += rows
    return place, multiplicity


WINDOW, MULTIPLICITY = window()
KROWS = len(MULTIPLICITY)

_at = 0


def _columns(n):
    global _at
    _at += n
    return slice(_at - n, _at)


C_IDENT = _columns(128)
C_IOTA = _columns(128)
C_BEFORE = _columns(128)
C_HEADS = _columns(HG)
C_FIRST = _columns(EXPERTS)
C_PAIR = _columns(PAIRS)
C_MEAN = _columns(1)
C_VALID = _columns(1)
C_JUNK = _columns(1)
C_TOKEN = _columns(1)
C_POWER = _columns(1)
C_EPS = _columns(1)
C_WIDTH = _at


def at_least(eng, sem, value):
    if not isinstance(value, int) or value > 0:
        eng.wait_ge(sem, value)


def pairs_loop(eng, body):
    def fixed(i):
        def pair(k):
            n = i + k
            return Step(n, n // 2, n % 2, n // 4, n % 4) if 0 <= n < PAIRS else None
        return pair

    def moving(j, u):
        def pair(k):
            c = 5 + u + k
            return Step(j * 4 + c, j * 2 + c // 2, c % 2, j + c // 4, c % 4)
        return pair

    for i in range(-3, 5):
        body(fixed(i))
    with eng.Fori(0, (PAIRS - 8) // 4) as j:
        for u in range(4):
            body(moving(j, u))
    for i in range(PAIRS - 3, PAIRS + 3):
        body(fixed(i))


def tiles_loop(eng, body):
    def fixed(i):
        def tile(k):
            n = i + k
            return Step(n, n // 2, n % 2, n // 4, n % 4) if 0 <= n < TILES else None
        return tile

    def moving(j, u):
        def tile(k):
            c = 5 + u + k
            return Step(j * 4 + c, j * 2 + c // 2, c % 2, j + c // 4, c % 4)
        return tile

    for i in range(-2, 5):
        body(fixed(i))
    with eng.Fori(0, (TILES - 8) // 4) as j:
        for u in range(4):
            body(moving(j, u))
    for i in range(TILES - 3, TILES + 1):
        body(fixed(i))


def build(nc, consts, xcol, wtok, gamma, beta, tok_b, wqkv, wproj, wrouter, w1, w2, b2, out):
    assert PAIRS % 4 == 0 and TILES % 4 == 0
    with ExitStack() as ctx:
        def sb(name, shape, dt=F32):
            return ctx.enter_context(nc.sbuf_tensor(name, shape, dt))

        def bank(name):
            return ctx.enter_context(nc.psum_tensor(name, [128, 512], F32))

        def sem(name):
            return ctx.enter_context(nc.semaphore(name))

        rows_dram = nc.dram_tensor("token_rows", [TOKENS, ROW], F32, kind="Internal").ap()
        out_rows = out.rearrange("b s d -> (b s) d")

        cst = sb("cst", [128, C_WIDTH])
        ident = cst[:, C_IDENT]
        wt_in = sb("wt_in", [KROWS, CHUNKS, SHIFTS, DIM])
        gam = sb("gam", [KROWS, CHUNKS, SHIFTS])
        bet = sb("bet", [KROWS, CHUNKS, SHIFTS])
        tokb = sb("tokb", [1, DIM])
        ones = sb("ones", [128, 128])
        weff = sb("weff", [KROWS, CHUNKS, DIM + 1])
        c1 = sb("c1", [128, DIM])
        c0 = sb("c0", [128, DIM])
        wqkv_sb = sb("wqkv_sb", [HALF + 1, 2, 3 * DIM])
        wproj_sb = sb("wproj_sb", [HALF + 1, 2, DIM])
        wrouter_sb = sb("wrouter_sb", [HALF + 1, 2, EXPERTS])
        w2_sb = sb("w2_sb", [128, EXPERTS, FT, DIM])
        b2_sb = sb("b2_sb", [128, EXPERTS, DIM])

        xt = [sb(f"xt{i}", [KROWS, CHUNKS, 128]) for i in range(2)]
        sq = sb("sq", [KROWS, CHUNKS * 2, SEQ])
        sqr = sb("sqr", [KROWS, 128])
        tok_st = sb("tok_st", [128, 2])
        tok_m2 = sb("tok_m2", [128, 1])
        tok_var = sb("tok_var", [128, 1])
        tok_rs = sb("tok_rs", [128, 1])
        h0 = [sb(f"h0_{i}", [128, DIM]) for i in range(4)]
        bn1, mv1, ve1, rs1 = (sb(n, [128, k]) for n, k in (("bn1", 6), ("mv1", 2), ("ve1", 1), ("rs1", 1)))
        bn2, mv2, ve2, rs2 = (sb(n, [128, k]) for n, k in (("bn2", 6), ("mv2", 2), ("ve2", 1), ("rs2", 1)))
        xn = [sb(f"xn{i}", [128, DIM]) for i in range(2)]
        xnT = sb("xnT", [HALF + 1, 2, 128])
        qk = sb("qk", [HALF, 2 * GROUPS, SPAN])
        km = sb("km", [HALF, GROUPS, 2, HG, SEQ])
        vb = [sb(f"vb{i}", [128, 2, HG, 2 * (DH + 1)]) for i in range(2)]
        ss = sb("ss", [128, GROUPS, HG, SEQ])
        smx = sb("smx", [128, GROUPS, HG])
        pr = sb("pr", [128, HEADS, SLOT])
        prT = sb("prT", [128, HG, 128])
        rden = sb("rden", [128, HG, 2])
        o = sb("o", [128, DIM])
        oT = sb("oT", [HALF + 1, 2, 128])
        row = [sb(f"row{i}", [128, ROW]) for i in range(2)]
        x2T = sb("x2T", [HALF + 1, 2, 128])
        logits = sb("logits", [128, PAIRS, EXPERTS])

        y_ps, t1_ps, t2_ps, qk_ps, v_ps, s0_ps, s1_ps, o_ps = (
            bank(n) for n in ("y_ps", "t1_ps", "t2_ps", "qk_ps", "v_ps", "s0_ps", "s1_ps", "o_ps"))
        s_ps = (s0_ps, s1_ps)

        r_mx = sb("r_mx", [128, PAIRS])
        r_sh = sb("r_sh", [128, PAIRS, EXPERTS])
        r_ex = sb("r_ex", [128, PAIRS, EXPERTS])
        r_den = sb("r_den", [128, PAIRS])
        r_prob = sb("r_prob", [128, PAIRS])
        r_eq = sb("r_eq", [128, PAIRS, EXPERTS])
        r_w = sb("r_w", [128, PAIRS, EXPERTS])
        r_wm = sb("r_wm", [128, PAIRS])
        r_oh = sb("r_oh", [128, PAIRS, EXPERTS])
        r_ohb = sb("r_ohb", [128, PAIRS, EXPERTS], BF16)
        before_b = sb("before_b", [128, 128], BF16)
        ones_b = sb("ones_b", [128, 128], BF16)
        iota_b = sb("iota_b", [128, 128], BF16)
        one1 = sb("one1", [128, EXPERTS * PAIRS])
        r_tot = sb("r_tot", [128, EXPERTS, PAIRS])
        r_cum = sb("r_cum", [128, EXPERTS, PAIRS])
        r_prev = sb("r_prev", [128, EXPERTS])
        r_cnt = sb("r_cnt", [128, EXPERTS], I32)
        r_nti = sb("r_nti", [128, EXPERTS], I32)
        r_nt = sb("r_nt", [128, EXPERTS])
        r_end = sb("r_end", [128, EXPERTS])
        r_start = sb("r_start", [128, EXPERTS])
        r_base = sb("r_base", [128, EXPERTS])
        r_off = sb("r_off", [128, EXPERTS, PAIRS])
        r_off2 = sb("r_off2", [128, EXPERTS, PAIRS])
        r_off3 = sb("r_off3", [128, PAIRS, EXPERTS])
        r_pos4 = sb("r_pos4", [128, PAIRS, EXPERTS])
        r_pos = sb("r_pos", [128, PAIRS], I32)
        r_modi = sb("r_modi", [128, PAIRS], I32)
        r_divi = sb("r_divi", [128, PAIRS], I32)
        r_mod = sb("r_mod", [128, PAIRS], BF16)
        r_div = sb("r_div", [128, PAIRS], BF16)
        r_ends = sb("r_ends", [128, TILES, EXPERTS])
        r_eidf = sb("r_eidf", [128, TILES])
        eid = sb("eid", [128, TILES], I32)
        vals = sb("vals", [128, PAIRS, VALUES], BF16)
        r_res = sb("r_res", [128, PAIRS])
        r_res2 = sb("r_res2", [128, PAIRS])
        slot_oh = sb("slot_oh", [128, PAIRS, 128], BF16)
        tile_oh = sb("tile_oh", [128, PAIRS, TILES], BF16)
        tile_v = sb("tile_v", [128, PAIRS, VALUES, TILES], BF16)
        got = sb("got", [128, VALUES, TILES])
        g_idx = sb("g_idx", [128, TILES])
        g_empty = sb("g_empty", [128, TILES])
        g_p12 = sb("g_p12", [128, TILES])
        prob = sb("prob", [128, TILES])
        gather_at = sb("gather_at", [128, TILES], U32)
        scatter_at = sb("scatter_at", [128, TILES], U32)

        w1s = [sb(f"w1s{i}", [HALF + 1, 2, FFN]) for i in range(2)]
        g = [sb(f"g{i}", [128, ROW]) for i in range(4)]
        gT = sb("gT", [HALF + 1, 2, 128])
        hT = [sb(f"hT{i}", [128, FT, TILE]) for i in range(2)]
        yb = sb("yb", [128, DIM])
        g_at = [sb(f"g_at{i}", [128, 1], U32) for i in range(4)]
        s_at = [sb(f"s_at{i}", [128, 1], U32) for i in range(2)]
        res = [sb(f"res{i}", [128, DIM]) for i in range(2)]

        consts_in, gb_in, wq_in, w2_in = sem("consts_in"), sem("gb_in"), sem("wq_in"), sem("w2_in")
        wt_in_sem = [sem(f"wt_in{c}") for c in range(CHUNKS)]
        init_done = sem("init_done")
        weff_step = sem("weff_step")
        c1_mm, c1_sb, centred = sem("c1_mm"), sem("c1_sb"), sem("centred")
        c0_mm, c0_sb = sem("c0_mm"), sem("c0_sb")
        x_in = [sem(f"x_in{i}") for i in range(2)]
        sq_done, sqr_done, tok_mm = sem("sq_done"), sem("sqr_done"), sem("tok_mm")
        st_done, m2_done, var_done, tok_rstd, h0_done = (
            sem("st_done"), sem("m2_done"), sem("var_done"), sem("tok_rstd"), sem("h0_done"))
        bn1_done, mv1_done, ve1_done, rs1_done, xn_done = (
            sem("bn1_done"), sem("mv1_done"), sem("ve1_done"), sem("rs1_done"), sem("xn_done"))
        t1_mm, xnT_done, qk_mm, v_mm, qk_sb, km_done, v_sb = (
            sem("t1_mm"), sem("xnT_done"), sem("qk_mm"), sem("v_mm"), sem("qk_sb"), sem("km_done"), sem("v_sb"))
        s_mm, smax, ssub, p_done, pt_mm, pt_sb = (
            sem("s_mm"), sem("smax"), sem("ssub"), sem("p_done"), sem("pt_mm"), sem("pt_sb"))
        pv_mm, rden_done, o_done, t2_mm, oT_done, pj_mm = (
            sem("pv_mm"), sem("rden_done"), sem("o_done"), sem("t2_mm"), sem("oT_done"), sem("pj_mm"))
        h1_done, bn2_done, mv2_done, ve2_done, rs2_done, xn2_done = (
            sem("h1_done"), sem("bn2_done"), sem("mv2_done"), sem("ve2_done"), sem("rs2_done"), sem("xn2_done"))
        row_out = [sem(f"row_out{i}") for i in range(2)]
        t3_mm, x2T_done, lg_mm, lg_done = sem("t3_mm"), sem("x2T_done"), sem("lg_mm"), sem("lg_done")
        r_step = sem("r_step")
        r_exp, r_counts, r_sb = sem("r_exp"), sem("r_counts"), sem("r_sb")
        r_slots, r_placed = sem("r_slots"), sem("r_placed")
        eid_done, idx_done = sem("eid_done"), sem("idx_done")
        w1_in = [sem(f"w1_in{i}") for i in range(2)]
        g_in = [sem(f"g_in{i}") for i in range(4)]
        gt_mm, gT_done, up_mm, gelu_done, down_mm = (
            sem("gt_mm"), sem("gT_done"), sem("up_mm"), sem("gelu_done"), sem("down_mm"))
        yb_done, res_done = sem("yb_done"), sem("res_done")
        g_at_done, s_at_done = sem("g_at_done"), sem("s_at_done")
        res_out = [sem(f"res_out{i}") for i in range(2)]

        waited = [sem("waited_dve"), sem("waited_pool")]

        def apart(eng):
            eng.sem_inc(waited[0 if eng is nc.vector else 1], 1)

        block = ctx.enter_context(nc.Block())

        def real(cols):
            return cols.rearrange("k (a t) -> k a t", a=2)[:, :, 0:SEQ]

        @block.sync
        def _(sp):
            for c in range(CHUNKS):
                sp.dma_start(wt_in[:, c], wtok[:, c]).then_inc(wt_in_sem[c], 16)

            def load_x(p):
                at_least(sp, tok_mm, p.n - 1)
                at_least(sp, sq_done, p.n - 1)
                src = xcol[bass.ds(p.n, 1)].rearrange("a k c t -> (a k) c t")
                sp.dma_start(xt[p.par][:], src).then_inc(x_in[p.par], 16)

            def store_rows(p):
                sp.wait_ge(xn2_done, p.n + 1)
                for a in range(2):
                    sp.dma_start(rows_dram[bass.ds(p.n * PAIR_TOKENS + a * SEQ, SEQ), :],
                                 row[p.par][a * SLOT:a * SLOT + SEQ, :]).then_inc(row_out[p.par], 16)

            def body(pair):
                if p := pair(3):
                    load_x(p)
                if p := pair(-3):
                    store_rows(p)

            pairs_loop(sp, body)

            sp.wait_ge(eid_done, 1)

            def tile_body(tile):
                if t := tile(2):
                    at_least(sp, up_mm, 2 * (t.n - 1))
                    e = sp.value_load(eid[0:1, bass.ds(t.n, 1)], min_val=0, max_val=EXPERTS - 1)
                    sp.dma_start(w1s[t.par][:], w1[bass.ds(e, 1)].rearrange("e k c f -> (e k) c f"))\
                        .then_inc(w1_in[t.par], 16)

            tiles_loop(sp, tile_body)
            for i in range(2):
                sp.wait_ge(row_out[i], 32 * (PAIRS // 2))
                sp.wait_ge(res_out[i], 16 * (TILES // 2))

        @block.tensor
        def _(pe):
            pe.wait_ge(init_done, 1)
            for c in range(CHUNKS):
                pe.wait_ge(weff_step, SHIFTS * (c + 1))
                mm = pe.matmul(t1_ps[:, 0:DIM], ones[0:KROWS, :], weff[:, c, 0:DIM],
                               start=(c == 0), stop=(c == CHUNKS - 1))
            mm.then_inc(c1_mm, 1)

            def fold_beta():
                pe.wait_ge(gb_in, 16 * 3)
                for c in range(CHUNKS):
                    for s in range(SHIFTS):
                        pe.matmul(t2_ps[:, 0:DIM], bet[:, c, s:s + 1].to_broadcast([KROWS, 128]),
                                  wt_in[:, c, s, :], start=(c == 0 and s == 0), stop=False)
                pe.matmul(t2_ps[:, 0:DIM], ones[0:1, :], tokb[:, :], start=False, stop=True).then_inc(c0_mm, 1)

            def tokens(p):
                pe.wait_ge(x_in[p.par], 16 * (p.half + 1))
                at_least(pe, h0_done, p.n)
                for c in range(CHUNKS):
                    if isinstance(p.n, int) and p.n == 0:
                        pe.wait_ge(centred, c + 1)
                    pe.matmul(y_ps[:, 0:DIM + 1], xt[p.par][:, c, :], weff[:, c, :],
                              start=(c == 0), stop=(c == CHUNKS - 1))
                pe.wait_ge(sqr_done, p.n + 1)
                pe.matmul(y_ps[:, DIM + 1:DIM + 2], sqr[:, :], cst[0:KROWS, C_MEAN],
                          start=True, stop=True).then_inc(tok_mm, 1)

            def turn(src, dst, n, ready, done):
                pe.wait_ge(ready, n + 1)
                for k in range(2):
                    mm = pe.transpose(dst[0:HALF, k * 128:(k + 1) * 128],
                                      src[:, k * HALF:(k + 1) * HALF], ident)
                mm.then_inc(done, 1)

            def project_qk(p):
                pe.wait_ge(xnT_done, p.n + 1)
                at_least(pe, qk_sb, p.n)
                for m in range(2 * GROUPS):
                    for k in range(2):
                        kr = HALF + 1 - k
                        mm = pe.matmul(qk_ps[0:HALF, m * PAIR_TOKENS:(m + 1) * PAIR_TOKENS],
                                       wqkv_sb[0:kr, k, m * HALF:(m + 1) * HALF], real(xnT[0:kr, k, :]),
                                       start=(k == 0), stop=(k == 1))
                mm.then_inc(qk_mm, 1)

            def project_v(p):
                at_least(pe, v_sb, p.n)
                for odd in range(2):
                    w = slice(2 * DIM + odd * HALF, 2 * DIM + (odd + 1) * HALF)
                    for a in range(2):
                        for k in range(2):
                            kr = HALF + 1 - k
                            mm = pe.matmul(v_ps[odd * SLOT:(odd + 1) * SLOT, a * HALF:(a + 1) * HALF],
                                           xnT[0:kr, k, a * SLOT:(a + 1) * SLOT], wqkv_sb[0:kr, k, w],
                                           start=(k == 0), stop=(k == 1))
                mm.then_inc(v_mm, 1)

            def scores(p):
                pe.wait_ge(km_done, p.n + 1)
                for gr in range(GROUPS):
                    at_least(pe, pt_sb, 2 * p.n - 1 + gr)
                    for a in range(2):
                        mm = pe.matmul(s_ps[gr][a * SLOT:(a + 1) * SLOT, 0:HG * SEQ],
                                       qk[:, 2 * gr, a * SEQ:a * SEQ + SLOT],
                                       km[:, gr, a].rearrange("k h t -> k (h t)"), start=True, stop=True)
                    mm.then_inc(s_mm, 1)

            def turn_probs(p):
                for gr in range(GROUPS):
                    pe.wait_ge(p_done, 2 * p.n + 1 + gr)
                    for i in range(HG // 2):
                        hp = gr * (HG // 2) + i
                        mm = pe.transpose(s_ps[gr][:, i * 128:(i + 1) * 128],
                                          pr[:, 2 * hp:2 * hp + 2, :].rearrange("p h t -> p (h t)"), ident)
                    mm.then_inc(pt_mm, 1)

            def mix(p):
                pe.wait_ge(v_sb, p.n + 1)
                at_least(pe, h1_done, p.n)
                for hp in range(HG):
                    if hp % (HG // 2) == 0:
                        pe.wait_ge(pt_sb, 2 * p.n + 1 + hp // (HG // 2))
                    for a in range(2):
                        mm = pe.matmul(o_ps[a * SLOT:(a + 1) * SLOT, hp * 34:(hp + 1) * 34],
                                       prT[:, hp, a * SLOT:(a + 1) * SLOT], vb[p.par][:, a, hp, :],
                                       start=True, stop=True)
                mm.then_inc(pv_mm, 1)

            def project(p):
                pe.wait_ge(oT_done, p.n + 1)
                for k in range(2):
                    kr = HALF + 1 - k
                    mm = pe.matmul(o_ps[:, 0:DIM], oT[0:kr, k, :], wproj_sb[0:kr, k, :],
                                   start=(k == 0), stop=(k == 1))
                mm.then_inc(pj_mm, 1)

            def router(p):
                pe.wait_ge(x2T_done, p.n + 1)
                at_least(pe, oT_done, clip(p.n + 2))
                for k in range(2):
                    kr = HALF + 1 - k
                    mm = pe.matmul(t2_ps[:, 0:EXPERTS], x2T[0:kr, k, :], wrouter_sb[0:kr, k, :],
                                   start=(k == 0), stop=(k == 1))
                mm.then_inc(lg_mm, 1)

            def clip(v):
                return min(v, PAIRS) if isinstance(v, int) else v

            def body(pair):
                if p := pair(0):
                    at_least(pe, x2T_done, p.n - 3)
                    turn(xn[p.par], t1_ps, p.n, xn_done, t1_mm)
                if p := pair(-1):
                    scores(p)
                if p := pair(-2):
                    at_least(pe, lg_done, p.n - 1)
                    turn(o, t2_ps, p.n, o_done, t2_mm)
                if p := pair(-3):
                    at_least(pe, xnT_done, clip(p.n + 4))
                    turn(row[p.par], t1_ps, p.n, xn2_done, t3_mm)
                if p := pair(0):
                    if isinstance(p.n, int) and p.n == 0:
                        pe.wait_ge(wq_in, 16 * 3)
                    project_qk(p)
                if p := pair(2):
                    tokens(p)
                    if isinstance(p.n, int) and p.n == 0:
                        fold_beta()
                if p := pair(-2):
                    project(p)
                if p := pair(-3):
                    router(p)
                if p := pair(-1):
                    turn_probs(p)
                if p := pair(0):
                    project_v(p)
                if p := pair(-1):
                    mix(p)

            pairs_loop(pe, body)

            pe.wait_ge(r_counts, 1)
            flat = r_ohb[:].rearrange("p a e -> p (a e)")
            pe.matmul(s_ps[0][:, 0:PAIRS * EXPERTS], before_b[:, :], flat, start=True, stop=True)
            pe.matmul(s_ps[1][:, 0:PAIRS * EXPERTS], ones_b[:, :], flat, start=True, stop=True)\
                .then_inc(r_sb, 1)
            for n in range(PAIRS):
                if n % 8 == 0:
                    pe.wait_ge(r_slots, n // 8 + 1)
                mm = pe.matmul(o_ps[:, 0:VALUES * TILES], slot_oh[:, n, :],
                               tile_v[:, n].rearrange("p v t -> p (v t)"),
                               start=(n == 0), stop=(n == PAIRS - 1))
            mm.then_inc(r_placed, 1)

            h_ps = ((s0_ps, s1_ps), (qk_ps, v_ps))
            out_ps = (y_ps, t2_ps)
            pe.wait_ge(w2_in, 32)

            def turn_rows(t):
                pe.wait_ge(g_in[t.ring], 16 * (t.quad + 1))
                at_least(pe, gT_done, t.n)
                for k in range(2):
                    mm = pe.transpose(t1_ps[0:HALF, k * 128:(k + 1) * 128],
                                      g[t.ring][:, k * HALF:(k + 1) * HALF], ident)
                mm.then_inc(gt_mm, 1)

            def up(t):
                pe.wait_ge(gT_done, t.n + 1)
                pe.wait_ge(w1_in[t.par], 16 * (t.half + 1))
                for hb in range(2):
                    at_least(pe, gelu_done, 2 * (t.n - 2) + 1 + hb)
                    for i in range(FH):
                        f = hb * FH + i
                        for k in range(2):
                            kr = HALF + 1 - k
                            mm = pe.matmul(h_ps[t.par][hb][:, i * TILE:(i + 1) * TILE],
                                           w1s[t.par][0:kr, k, f * 128:(f + 1) * 128], gT[0:kr, k, :],
                                           start=(k == 0), stop=(k == 1))
                    mm.then_inc(up_mm, 1)

            def down(t):
                e = pe.value_load(eid[0:1, bass.ds(t.n, 1)], min_val=0, max_val=EXPERTS - 1)
                at_least(pe, yb_done, t.n - 1)
                for f in range(FT):
                    if f % FH == 0:
                        pe.wait_ge(gelu_done, 2 * t.n + 1 + f // FH)
                    mm = pe.matmul(out_ps[t.par][:, 0:DIM], hT[t.par][:, f, :],
                                   w2_sb[:, bass.ds(e, 1), f, :].rearrange("p e d -> p (e d)"),
                                   start=(f == 0), stop=(f == FT - 1))
                mm.then_inc(down_mm, 1)

            def tile_body(tile):
                if t := tile(0):
                    up(t)
                if t := tile(1):
                    turn_rows(t)
                if t := tile(-1):
                    down(t)

            pe.wait_ge(eid_done, 1)
            tiles_loop(pe, tile_body)

        @block.scalar
        def _(act):
            act.dma_start(cst[:], consts).then_inc(consts_in, 16)
            act.dma_start(gam[:], gamma).then_inc(gb_in, 16)
            act.dma_start(bet[:], beta).then_inc(gb_in, 16)
            act.dma_start(tokb[:], tok_b.rearrange("(a d) -> a d", a=1)).then_inc(gb_in, 16)
            act.dma_start(wqkv_sb[:], wqkv).then_inc(wq_in, 16)
            act.dma_start(wproj_sb[:], wproj).then_inc(wq_in, 16)
            act.dma_start(wrouter_sb[:], wrouter).then_inc(wq_in, 16)

            def square(p):
                act.wait_ge(x_in[p.par], 16 * (p.half + 1))
                at_least(act, sqr_done, p.n)
                act.activation(sq[:], xt[p.par][:].rearrange("k c (a t) -> k (c a) t", a=2)[:, :, 0:SEQ],
                               ACT.Square).then_inc(sq_done, 1)

            def copy_turned(dst, src, ready, used, n, done):
                act.wait_ge(ready, n + 1)
                at_least(act, used, n)
                act.copy(dst[0:HALF, :, :].rearrange("k a t -> k (a t)"), src[0:HALF, 0:256]).then_inc(done, 1)

            def exps(p, gr):
                act.wait_ge(ssub, 2 * p.n + 1 + gr)
                at_least(act, pt_mm, 2 * p.n - 1 + gr)
                act.activation(pr[:, gr * HG:(gr + 1) * HG, 0:SEQ], ss[:, gr], ACT.Exp,
                               scale=float(DH) ** -0.5).then_inc(p_done, 1)

            def copy_qk(p):
                act.wait_ge(qk_mm, p.n + 1)
                at_least(act, s_mm, 2 * p.n)
                at_least(act, km_done, p.n)
                act.copy(qk[:, :, 0:PAIR_TOKENS],
                         qk_ps[0:HALF, 0:4 * PAIR_TOKENS].rearrange("k (m t) -> k m t", m=4)).then_inc(qk_sb, 1)

            def copy_probs(p):
                at_least(act, pv_mm, p.n)
                for gr in range(GROUPS):
                    act.wait_ge(pt_mm, 2 * p.n + 1 + gr)
                    act.copy(prT[:, gr * 3:gr * 3 + 3, :].rearrange("p h s -> p (h s)"),
                             s_ps[gr][:, 0:384]).then_inc(pt_sb, 1)

            act.wait_ge(init_done, 1)

            def body(pair):
                if p := pair(0):
                    copy_turned(xnT, t1_ps, t1_mm, v_mm, p.n, xnT_done)
                if p := pair(-2):
                    copy_turned(oT, t2_ps, t2_mm, pj_mm, p.n, oT_done)
                if p := pair(-3):
                    copy_turned(x2T, t1_ps, t3_mm, lg_mm, p.n, x2T_done)
                if p := pair(-1):
                    exps(p, 0)
                if p := pair(0):
                    copy_qk(p)
                if p := pair(-1):
                    exps(p, 1)
                if p := pair(3):
                    square(p)
                if p := pair(-1):
                    copy_probs(p)

            pairs_loop(act, body)

            act.wait_ge(r_exp, 1)
            act.activation(r_ex[:], r_sh[:], ACT.Exp).then_inc(r_exp, 1)

            def gelus(t):
                h_ps = ((s0_ps, s1_ps), (qk_ps, v_ps))
                at_least(act, down_mm, t.n - 1)
                for hb in range(2):
                    act.wait_ge(up_mm, 2 * t.n + 1 + hb)
                    act.activation(hT[t.par][:, hb * FH:(hb + 1) * FH, :].rearrange("p f t -> p (f t)"),
                                   h_ps[t.par][hb][:, 0:FH * TILE], ACT.Gelu).then_inc(gelu_done, 1)

            def copy_rows(t):
                act.wait_ge(gt_mm, t.n + 1)
                at_least(act, up_mm, 2 * t.n)
                act.copy(gT[0:HALF, :, :].rearrange("k a t -> k (a t)"), t1_ps[0:HALF, 0:256]).then_inc(gT_done, 1)

            def tile_body(tile):
                if t := tile(0):
                    gelus(t)
                if t := tile(1):
                    copy_rows(t)

            tiles_loop(act, tile_body)

        @block.gpsimd
        def _(pool):
            pool.wait_ge(init_done, 1)
            pool.wait_ge(consts_in, 16)

            def mask_k(p):
                pool.wait_ge(qk_sb, p.n + 1)
                at_least(pool, s_mm, 2 * p.n)
                heads = cst[0:HALF, C_HEADS].unsqueeze(2).to_broadcast([HALF, HG, SEQ])
                for gr in range(GROUPS):
                    for a in range(2):
                        k = qk[:, 2 * gr + 1, a * SEQ:(a + 1) * SEQ].unsqueeze(1).to_broadcast([HALF, HG, SEQ])
                        last = pool.tensor_tensor(km[:, gr, a], k, heads, ALU.mult)
                last.then_inc(km_done, 1)

            def inverse_deviation(mv, ve, rs, n, ready, ve_sem, done):
                pool.wait_ge(ready, n + 1)
                pool.tensor_tensor(ve[:], mv[:, 1:2], cst[:, C_EPS], ALU.add).then_inc(ve_sem, 1)
                pool.wait_ge(ve_sem, n + 1)
                pool.tensor_tensor(rs[:], ve[:], cst[:, C_POWER], ALU.pow).then_inc(done, 1)

            def token_deviation(p):
                pool.wait_ge(st_done, p.n + 1)
                pool.tensor_tensor(tok_m2[:], tok_st[:, 0:1], tok_st[:, 0:1], ALU.mult).then_inc(m2_done, 1)
                pool.wait_ge(m2_done, p.n + 1)
                pool.tensor_tensor(tok_var[:], tok_st[:, 1:2], tok_m2[:], ALU.subtract).then_inc(var_done, 1)
                pool.wait_ge(var_done, p.n + 1)
                pool.tensor_tensor(tok_rs[:], tok_var[:], cst[:, C_POWER], ALU.pow).then_inc(tok_rstd, 1)

            def body(pair):
                if p := pair(0):
                    mask_k(p)
                if p := pair(2):
                    token_deviation(p)
                if p := pair(-2):
                    inverse_deviation(mv2, ve2, rs2, p.n, mv2_done, ve2_done, rs2_done)
                if p := pair(2):
                    inverse_deviation(mv1, ve1, rs1, p.n, mv1_done, ve1_done, rs1_done)
                if (p := pair(0)) and isinstance(p.n, int) and p.n == 2:
                    pool.dma_start(w2_sb[:], w2).then_inc(w2_in, 16)
                    pool.dma_start(b2_sb[:], b2.unsqueeze(0).to_broadcast([128, EXPERTS, DIM])).then_inc(w2_in, 16)

            pairs_loop(pool, body)

            pool.wait_ge(idx_done, 1)
            for i in range(2):
                pool.wait_ge(row_out[i], 32 * (PAIRS // 2))

            def gather(t):
                at_least(pool, res_done, t.n - 3)
                apart(pool)
                pool.tensor_copy(g_at[t.ring][:], gather_at[:, bass.ds(t.n, 1)]).then_inc(g_at_done, 1)
                pool.wait_ge(g_at_done, t.n + 1)
                apart(pool)
                pool.indirect_dma_start(g[t.ring][:, :], None, rows_dram[:, :],
                                        bass.IndirectOffsetOnAxis(ap=g_at[t.ring][:, 0:1], axis=0))\
                    .then_inc(g_in[t.ring], 16)

            def scatter(t):
                pool.wait_ge(res_done, t.n + 1)
                at_least(pool, res_out[t.par], t.half * 16)
                apart(pool)
                pool.tensor_copy(s_at[t.par][:], scatter_at[:, bass.ds(t.n, 1)]).then_inc(s_at_done, 1)
                pool.wait_ge(s_at_done, t.n + 1)
                apart(pool)
                pool.indirect_dma_start(out_rows, bass.IndirectOffsetOnAxis(ap=s_at[t.par][:, 0:1], axis=0),
                                        res[t.par][:, :], None, bounds_check=TOKENS - 1, oob_is_err=False)\
                    .then_inc(res_out[t.par], 16)

            def tile_body(tile):
                if t := tile(3):
                    gather(t)
                if t := tile(-1):
                    scatter(t)

            gather(Step(0, 0, 0, 0, 0))
            tiles_loop(pool, tile_body)

        @block.vector
        def _(dve):
            dve.memset(ones[:], 1.0)
            dve.memset(ones_b[:], 1.0)
            dve.memset(one1[:], 1.0)
            for x in (xnT, oT, x2T, gT):
                dve.memset(x[HALF:HALF + 1, :, :], 1.0)
            dve.memset(qk[:, :, PAIR_TOKENS:SPAN], 0.0)
            dve.memset(pr[:, :, SEQ:SLOT], 0.0)
            dve.memset(r_prev[:, 0:1], 0.0)
            dve.memset(sqr[:], 0.0)
            for v in vb:
                dve.memset(v[0:SLOT, :, :, DH + 1:2 * DH + 2], 0.0)
                dve.memset(v[SLOT:128, :, :, 0:DH + 1], 0.0)
                dve.memset(v[0:SLOT, :, :, DH:DH + 1], 1.0)
                last = dve.memset(v[SLOT:128, :, :, 2 * DH + 1:2 * DH + 2], 1.0)
            last.then_inc(init_done, 1)

            dve.wait_ge(gb_in, 16 * 3)
            step = 0
            for c in range(CHUNKS):
                dve.wait_ge(wt_in_sem[c], 16)
                for s in range(SHIFTS):
                    if s == 0:
                        ins = dve.tensor_scalar(weff[:, c, 0:DIM], wt_in[:, c, s, :], gam[:, c, s:s + 1], None, ALU.mult)
                    else:
                        dve.wait_ge(weff_step, step)
                        ins = dve.scalar_tensor_tensor(out=weff[:, c, 0:DIM], in0=wt_in[:, c, s, :],
                                                       scalar=gam[:, c, s:s + 1], in1=weff[:, c, 0:DIM],
                                                       op0=ALU.mult, op1=ALU.add)
                    ins.then_inc(weff_step, 1)
                    step += 1
            dve.wait_ge(consts_in, 16)
            dve.wait_ge(c1_mm, 1)
            dve.tensor_scalar(c1[:], t1_ps[:, 0:DIM], cst[:, C_MEAN], None, ALU.mult).then_inc(c1_sb, 1)
            dve.wait_ge(c1_sb, 1)
            for c in range(CHUNKS):
                dve.tensor_copy(weff[:, c, DIM:DIM + 1], cst[0:KROWS, C_MEAN])
                dve.tensor_tensor(weff[:, c, 0:DIM], weff[:, c, 0:DIM], c1[0:KROWS, :], ALU.subtract)\
                    .then_inc(centred, 1)
            dve.tensor_copy(before_b[:], cst[:, C_BEFORE])
            dve.tensor_copy(iota_b[:], cst[:, C_IOTA])

            def normalise_mix(p):
                dve.wait_ge(pv_mm, p.n + 1)
                v = o_ps[:, 0:HEADS * (DH + 1)].rearrange("p (h d) -> p h d", h=HEADS)
                dve.reciprocal(rden[:].rearrange("p a b -> p (a b)"), v[:, :, DH]).then_inc(rden_done, 1)
                dve.wait_ge(rden_done, p.n + 1)
                at_least(dve, t2_mm, p.n)
                dve.tensor_tensor(o[:].rearrange("p (h d) -> p h d", h=HEADS), v[:, :, 0:DH],
                                  rden[:].rearrange("p a b -> p (a b)").unsqueeze(2).to_broadcast([128, HEADS, DH]),
                                  ALU.mult).then_inc(o_done, 1)

            def sum_squares(p):
                dve.wait_ge(sq_done, p.n + 1)
                at_least(dve, tok_mm, p.n)
                dve.tensor_reduce(real(sqr[:, :]), sq[:].rearrange("k (c a) t -> k a t c", a=2), AX, ALU.add).then_inc(sqr_done, 1)

            def shift_scores(p):
                for gr in range(GROUPS):
                    dve.wait_ge(s_mm, 2 * p.n + 1 + gr)
                    v = s_ps[gr][:, 0:HG * SEQ].rearrange("p (h t) -> p h t", h=HG)
                    dve.tensor_reduce(smx[:, gr], v, AX, ALU.max).then_inc(smax, 1)
                    dve.wait_ge(smax, 2 * p.n + 1 + gr)
                    at_least(dve, p_done, 2 * p.n - 1 + gr)
                    dve.tensor_tensor(ss[:, gr], v, smx[:, gr].unsqueeze(2).to_broadcast([128, HG, SEQ]),
                                      ALU.subtract).then_inc(ssub, 1)

            def copy_logits(p):
                dve.wait_ge(lg_mm, p.n + 1)
                dve.tensor_copy(logits[:, bass.ds(p.n, 1), :].rearrange("p a e -> p (a e)"),
                                t2_ps[:, 0:EXPERTS]).then_inc(lg_done, 1)

            def copy_v(p):
                dve.wait_ge(v_mm, p.n + 1)
                at_least(dve, pv_mm, p.n - 1)
                v = v_ps[:, 0:DIM].rearrange("p (a h d) -> p a h d", a=2, h=HG)
                dve.tensor_copy(vb[p.par][0:SLOT, :, :, 0:DH], v[0:SLOT])
                dve.tensor_copy(vb[p.par][SLOT:128, :, :, DH + 1:2 * DH + 1], v[SLOT:128])\
                    .then_inc(v_sb, 1)

            def statistics(p, src, bn, mv, src_done, bn_sem, mv_sem):
                dve.wait_ge(src_done, p.n + 1)
                dve.bn_stats(bn[:], src).then_inc(bn_sem, 1)
                dve.wait_ge(bn_sem, p.n + 1)
                apart(dve)
                dve.bn_aggr(mv[:], bn[:]).then_inc(mv_sem, 1)

            def add_residual(p):
                dve.wait_ge(pj_mm, p.n + 1)
                at_least(dve, row_out[p.par], p.half * 32)
                at_least(dve, t3_mm, p.n - 1)
                dve.tensor_tensor(row[p.par][:, DIM:ROW], o_ps[:, 0:DIM], h0[p.ring][:], ALU.add).then_inc(h1_done, 1)
                statistics(p, row[p.par][:, DIM:ROW], bn2, mv2, h1_done, bn2_done, mv2_done)

            def second_norm(p):
                dve.wait_ge(mv2_done, p.n + 1)
                dve.wait_ge(rs2_done, p.n + 1)
                dve.tensor_scalar(row[p.par][:, 0:DIM], row[p.par][:, DIM:ROW], mv2[:, 0:1], rs2[:, 0:1],
                                  ALU.subtract, ALU.mult).then_inc(xn2_done, 1)

            def token_statistics(p):
                dve.wait_ge(tok_mm, p.n + 1)
                dve.tensor_copy(tok_st[:, 0:1], y_ps[:, DIM:DIM + 1])
                dve.tensor_scalar(tok_st[:, 1:2], y_ps[:, DIM + 1:DIM + 2], LN_EPS, None, ALU.add).then_inc(st_done, 1)

            def embed(p):
                dve.wait_ge(tok_rstd, p.n + 1)
                at_least(dve, h1_done, p.n - 3)
                dve.scalar_tensor_tensor(out=h0[p.ring][:], in0=y_ps[:, 0:DIM], scalar=tok_rs[:, 0:1], in1=c0[:],
                                         op0=ALU.mult, op1=ALU.add).then_inc(h0_done, 1)
                statistics(p, h0[p.ring][:], bn1, mv1, h0_done, bn1_done, mv1_done)

            def first_norm(p):
                dve.wait_ge(mv1_done, p.n + 1)
                at_least(dve, t1_mm, p.n - 1)
                dve.wait_ge(rs1_done, p.n + 1)
                dve.tensor_scalar(xn[p.par][:], h0[p.ring][:], mv1[:, 0:1], rs1[:, 0:1],
                                  ALU.subtract, ALU.mult).then_inc(xn_done, 1)

            def body(pair):
                if p := pair(-2):
                    normalise_mix(p)
                if p := pair(-1):
                    shift_scores(p)
                if p := pair(2):
                    token_statistics(p)
                if p := pair(3):
                    sum_squares(p)
                if p := pair(-2):
                    add_residual(p)
                if p := pair(2):
                    if isinstance(p.n, int) and p.n == 0:
                        dve.wait_ge(c0_mm, 1)
                        dve.tensor_copy(c0[:], t2_ps[:, 0:DIM]).then_inc(c0_sb, 1)
                        dve.wait_ge(c0_sb, 1)
                    embed(p)
                if p := pair(-3):
                    copy_logits(p)
                if p := pair(-2):
                    second_norm(p)
                if p := pair(0):
                    copy_v(p)
                if p := pair(2):
                    first_norm(p)

            pairs_loop(dve, body)

            done = [0]

            def step_(ins):
                done[0] += 1
                ins.then_inc(r_step, 1)
                dve.wait_ge(r_step, done[0])

            def over_experts(x):
                return x.unsqueeze(2).to_broadcast([128, PAIRS, EXPERTS])

            dve.wait_ge(lg_done, PAIRS)
            step_(dve.tensor_reduce(r_mx[:], logits[:], AX, ALU.max))
            dve.tensor_tensor(r_sh[:], logits[:], over_experts(r_mx[:]), ALU.subtract).then_inc(r_exp, 1)
            step_(dve.tensor_tensor(r_eq[:], logits[:], over_experts(r_mx[:]), ALU.is_equal))
            step_(dve.tensor_tensor(r_w[:], r_eq[:],
                                    cst[:, C_FIRST].unsqueeze(1).to_broadcast([128, PAIRS, EXPERTS]), ALU.mult))
            step_(dve.tensor_reduce(r_wm[:], r_w[:], AX, ALU.max))
            step_(dve.tensor_tensor(r_oh[:], r_w[:], over_experts(r_wm[:]), ALU.is_equal))
            step_(dve.tensor_scalar(r_oh[:], r_oh[:], cst[:, C_VALID], None, ALU.mult))
            dve.tensor_copy(r_ohb[:], r_oh[:]).then_inc(r_counts, 1)
            dve.wait_ge(r_exp, 2)
            step_(dve.tensor_reduce(r_den[:], r_ex[:], AX, ALU.add))
            step_(dve.reciprocal(r_prob[:], r_den[:]))
            step_(dve.tensor_copy(vals[:, :, 2], r_prob[:]))
            step_(dve.tensor_tensor(r_res[:], r_prob[:], vals[:, :, 2], ALU.subtract))
            step_(dve.tensor_copy(vals[:, :, 3], r_res[:]))
            step_(dve.tensor_tensor(r_res2[:], r_res[:], vals[:, :, 3], ALU.subtract))
            dve.tensor_copy(vals[:, :, 4], r_res2[:])
            dve.tensor_copy(vals[:, :, 0], cst[:, C_TOKEN].to_broadcast([128, PAIRS]))
            step_(dve.tensor_copy(vals[:, :, 1], cst[:, C_PAIR]))
            dve.wait_ge(r_sb, 1)
            before = s_ps[0][:, 0:PAIRS * EXPERTS].rearrange("p (a e) -> p a e", e=EXPERTS)
            total = s_ps[1][:, 0:PAIRS * EXPERTS].rearrange("p (a e) -> p e a", e=EXPERTS)
            step_(dve.tensor_copy(r_tot[:], total))
            step_(dve.tensor_tensor_scan(r_cum[:].rearrange("p e a -> p (e a)"), one1[:],
                                         r_tot[:].rearrange("p e a -> p (e a)"), 0.0, ALU.mult, ALU.add))
            ends = r_cum[:, :, PAIRS - 1]
            step_(dve.tensor_copy(r_prev[:, 1:EXPERTS], r_cum[:, 0:EXPERTS - 1, PAIRS - 1]))
            step_(dve.scalar_tensor_tensor(out=r_cnt[:], in0=ends, scalar=float(TILE - 1), in1=r_prev[:],
                                           op0=ALU.add, op1=ALU.subtract))
            step_(dve.tensor_scalar(r_nti[:], r_cnt[:], 7, None, ALU.logical_shift_right))
            step_(dve.tensor_copy(r_nt[:], r_nti[:]))
            step_(dve.tensor_tensor_scan(r_end[:], one1[:, 0:EXPERTS], r_nt[:], 0.0, ALU.mult, ALU.add))
            step_(dve.tensor_tensor(r_ends[:], r_end[:].unsqueeze(1).to_broadcast([128, TILES, EXPERTS]),
                                    cst[:, C_IOTA][:, 0:TILES].unsqueeze(2).to_broadcast([128, TILES, EXPERTS]),
                                    ALU.is_le))
            step_(dve.tensor_reduce(r_eidf[:], r_ends[:], AX, ALU.add))
            dve.tensor_scalar(eid[:], r_eidf[:], float(EXPERTS - 1), None, ALU.min).then_inc(eid_done, 1)
            step_(dve.tensor_tensor(r_start[:], r_end[:], r_nt[:], ALU.subtract))
            step_(dve.scalar_tensor_tensor(out=r_base[:], in0=r_start[:], scalar=float(TILE), in1=r_prev[:],
                                           op0=ALU.mult, op1=ALU.subtract))
            step_(dve.tensor_tensor(r_off[:], r_cum[:], r_tot[:], ALU.subtract))
            step_(dve.tensor_tensor(r_off2[:], r_off[:], r_base[:].unsqueeze(2).to_broadcast([128, EXPERTS, PAIRS]),
                                    ALU.add))
            step_(dve.tensor_tensor(r_off3[:], before, r_off2[:].rearrange("p e a -> p a e"), ALU.add))
            step_(dve.tensor_tensor(r_pos4[:], r_off3[:], r_oh[:], ALU.mult))
            step_(dve.tensor_reduce(r_den[:], r_pos4[:], AX, ALU.add))
            step_(dve.tensor_copy(r_pos[:], r_den[:]))
            dve.tensor_scalar(r_modi[:], r_pos[:], TILE - 1, None, ALU.bitwise_and)
            step_(dve.tensor_scalar(r_divi[:], r_pos[:], 7, None, ALU.logical_shift_right))
            dve.tensor_copy(r_mod[:], r_modi[:])
            step_(dve.scalar_tensor_tensor(out=r_div[:], in0=r_divi[:], scalar=1.0,
                                           in1=cst[:, C_JUNK].to_broadcast([128, PAIRS]),
                                           op0=ALU.mult, op1=ALU.add))
            step_(dve.tensor_tensor(tile_oh[:], r_div[:].unsqueeze(2).to_broadcast([128, PAIRS, TILES]),
                                    iota_b[:, 0:TILES].unsqueeze(1).to_broadcast([128, PAIRS, TILES]), ALU.is_equal))
            for n in range(0, PAIRS, 8):
                dve.tensor_tensor(slot_oh[:, n:n + 8, :], r_mod[:, n:n + 8].unsqueeze(2).to_broadcast([128, 8, 128]),
                                  iota_b[:].unsqueeze(1).to_broadcast([128, 8, 128]), ALU.is_equal)
                for v in range(VALUES):
                    ins = dve.tensor_tensor(tile_v[:, n:n + 8, v, :], tile_oh[:, n:n + 8, :],
                                            vals[:, n:n + 8, v].unsqueeze(2).to_broadcast([128, 8, TILES]), ALU.mult)
                ins.then_inc(r_slots, 1)
            dve.wait_ge(r_placed, 1)
            step_(dve.tensor_copy(got[:], o_ps[:, 0:VALUES * TILES].rearrange("p (v t) -> p v t", v=VALUES)))
            dve.tensor_scalar(g_empty[:], got[:, 0], 0.0, float(SKIP), ALU.is_equal, ALU.mult)
            dve.tensor_tensor(g_p12[:], got[:, 2], got[:, 3], ALU.add)
            step_(dve.scalar_tensor_tensor(out=g_idx[:], in0=got[:, 1], scalar=float(PAIR_TOKENS), in1=got[:, 0],
                                           op0=ALU.mult, op1=ALU.add))
            dve.tensor_tensor(prob[:], g_p12[:], got[:, 4], ALU.add)
            dve.tensor_scalar(gather_at[:], g_idx[:], -1.0, 0.0, ALU.add, ALU.max)
            dve.scalar_tensor_tensor(out=scatter_at[:], in0=g_idx[:], scalar=-1.0, in1=g_empty[:],
                                     op0=ALU.add, op1=ALU.add).then_inc(idx_done, 1)

            out_ps = (y_ps, t2_ps)
            dve.wait_ge(w2_in, 32)

            def tile_body(tile):
                if t := tile(-1):
                    e = dve.value_load(eid[0:1, bass.ds(t.n, 1)], min_val=0, max_val=EXPERTS - 1)
                    dve.wait_ge(down_mm, t.n + 1)
                    at_least(dve, res_done, t.n)
                    dve.tensor_tensor(yb[:], out_ps[t.par][:, 0:DIM],
                                      b2_sb[:, bass.ds(e, 1), :].rearrange("p e d -> p (e d)"), ALU.add).then_inc(yb_done, 1)
                    dve.wait_ge(yb_done, t.n + 1)
                    at_least(dve, res_out[t.par], t.half * 16)
                    dve.scalar_tensor_tensor(out=res[t.par][:], in0=yb[:], scalar=prob[:, bass.ds(t.n, 1)],
                                             in1=g[t.ring][:, DIM:ROW], op0=ALU.mult, op1=ALU.add).then_inc(res_done, 1)

            tiles_loop(dve, tile_body)


def constants():
    import numpy as np

    c = np.zeros((128, C_WIDTH), np.float32)
    p = np.arange(128)
    c[:, C_IDENT] = np.eye(128)
    c[:, C_IOTA] = p[None, :]
    c[:, C_BEFORE] = p[:, None] < p[None, :]
    c[:, C_HEADS] = p[:, None] // DH == np.arange(HG)[None, :]
    c[:, C_FIRST] = EXPERTS - np.arange(EXPERTS)[None, :]
    c[:, C_PAIR] = np.arange(PAIRS)[None, :]
    c[:KROWS, C_MEAN] = np.asarray(MULTIPLICITY, np.float64)[:, None] / PATCH_DIM
    c[:, C_VALID] = (p % SLOT < SEQ)[:, None]
    c[:, C_JUNK] = (p % SLOT >= SEQ)[:, None] * 64.0
    c[:, C_TOKEN] = (p // SLOT * SEQ + p % SLOT + 1)[:, None]
    c[:, C_POWER] = -0.5
    c[:, C_EPS] = LN_EPS
    return c


def lay_out(inputs):
    import numpy as np

    a = {k: np.asarray(v) for k, v in inputs.items()}
    x = a["x"]
    f32 = x.dtype
    padded = np.zeros((IMAGES, CH, SIDE + 2, SIDE + 2), f32)
    padded[:, :, 1:-1, 1:-1] = x
    tokens = np.zeros((KROWS, CHUNKS, TOKENS), f32)
    for (r, q, c), (chunk, k) in WINDOW.items():
        v = padded[:, c, r + 1:r + 1 + SIDE:PATCH, q + 1:q + 1 + SIDE:PATCH]
        tokens[k, chunk] = v[:, :GRID, :GRID].reshape(-1)
    xcol = np.zeros((PAIRS, KROWS, CHUNKS, 2, SLOT), f32)
    xcol[..., :SEQ] = tokens.reshape(KROWS, CHUNKS, PAIRS, 2, SEQ).transpose(2, 0, 1, 3, 4)
    xcol = xcol.reshape(PAIRS, KROWS, CHUNKS, 128)

    moves = ((0, 0), (0, -1), (0, 1), (-1, 0), (1, 0))
    w = a["L0_tok_W"].reshape(PATCH, PATCH, SHIFTS, CH, DIM)
    gb = [a[n].reshape(PATCH, PATCH, SHIFTS, CH) for n in ("L0_tok_ln_gamma", "L0_tok_ln_beta")]
    wtok = np.zeros((KROWS, CHUNKS, SHIFTS, DIM), f32)
    gamma, beta = (np.zeros((KROWS, CHUNKS, SHIFTS), f32) for _ in range(2))
    for (r, q, c), (chunk, k) in WINDOW.items():
        for s, (dr, dq) in enumerate(moves):
            ph, pw = r - dr, q - dq
            if 0 <= ph < PATCH and 0 <= pw < PATCH:
                wtok[k, chunk, s] = w[ph, pw, s, c]
                gamma[k, chunk, s] = gb[0][ph, pw, s, c]
                beta[k, chunk, s] = gb[1][ph, pw, s, c]

    def halves(weight, bias):
        m = np.zeros((HALF + 1, 2, weight.shape[1]), f32)
        m[:HALF] = weight.reshape(2, HALF, -1).transpose(1, 0, 2)
        m[HALF, 0] = bias
        return m

    def qkv_order(m):
        q, k, v = m[..., :DIM], m[..., DIM:2 * DIM], m[..., 2 * DIM:]
        v = v.reshape(v.shape[:-1] + (HG, 2, DH)).swapaxes(-3, -2).reshape(v.shape)
        return np.concatenate([q[..., :HALF], k[..., :HALF], q[..., HALF:], k[..., HALF:], v], axis=-1)

    return {
        "consts": constants(),
        "xcol": xcol,
        "wtok": wtok,
        "gamma": gamma,
        "beta": beta,
        "tok_b": a["L0_tok_b"],
        "wqkv": halves(qkv_order(a["L0_attn_w_attn"]), qkv_order(a["L0_attn_b_attn"])),
        "wproj": halves(a["L0_attn_w_proj"], a["L0_attn_b_proj"]),
        "wrouter": halves(a["L0_ffn_Ws"], a["L0_ffn_bs"]),
        "w1": np.stack([halves(a["L0_ffn_W1"][e], a["L0_ffn_b1"][e]) for e in range(EXPERTS)]),
        "w2": np.ascontiguousarray(a["L0_ffn_W2"].reshape(EXPERTS, FT, 128, DIM).transpose(2, 0, 1, 3)),
        "b2": a["L0_ffn_b2"],
    }


def kernel(**inputs):
    import numpy as np
    import concourse.bacc as bacc
    from concourse.bass_utils import run_bass_kernel_spmd

    nc = bacc.Bacc("TRN2", target_bir_lowering=False, num_devices=1)
    arrays = {k: np.ascontiguousarray(v) for k, v in lay_out(inputs).items()}
    args = [nc.dram_tensor(k, v.shape, mybir.dt.from_np(v.dtype), kind="ExternalInput").ap()
            for k, v in arrays.items()]
    out = nc.dram_tensor("out", (IMAGES, SEQ, DIM), F32, kind="ExternalOutput").ap()
    build(nc, *args, out)
    r = run_bass_kernel_spmd(nc, [arrays], core_ids=[0])
    return r.results[0]["out"]
```

```python
from collections import namedtuple
from contextlib import ExitStack

import concourse.bass as bass
from concourse import mybir
from concourse.alu_op_type import AluOpType as ALU

F32 = mybir.dt.float32
BF16 = mybir.dt.bfloat16
I32 = mybir.dt.int32
U32 = mybir.dt.uint32
ACT = mybir.ActivationFunctionType
AX = mybir.AxisListType.X

IMAGES, CH, SIDE, PATCH = 64, 3, 112, 16
GRID = SIDE // PATCH
SEQ = GRID * GRID
TOKENS = IMAGES * SEQ
DIM = 192
HALF = DIM // 2
HEADS, DH = 12, 16
GROUPS, HG = 2, 6
EXPERTS, FFN = 8, 768
SHIFTS = 5
PATCH_DIM = PATCH * PATCH * SHIFTS * CH
LN_EPS = 1e-5

PAIRS = IMAGES // 2
SLOT = 64
PAIR_TOKENS = 2 * SEQ
SPAN = SEQ + SLOT

BLOCKS = -(-TOKENS // 128)
LAST_ROWS = TOKENS - (BLOCKS - 1) * 128

CHUNKS = 8
MULTIPLICITIES = (5, 4, 3, 1)

TILE = 128
TILES = (TOKENS + EXPERTS * (TILE - 1)) // TILE
FT = FFN // 128
FH = FT // 2
ROW = 2 * DIM
VALUES = 5
INDEX, PROB = slice(0, 2), slice(2, 5)
SKIP = 8192

Step = namedtuple("Step", "n half par quad ring")


def window():
    pixels = []
    for r in range(-1, PATCH + 1):
        for q in range(-1, PATCH + 1):
            if 0 <= r < PATCH or 0 <= q < PATCH:
                m = sum(0 <= r + dr < PATCH and 0 <= q + dq < PATCH
                        for dr, dq in ((0, 0), (0, 1), (0, -1), (1, 0), (-1, 0)))
                pixels += [(m, r, q, c) for c in range(CH)]
    place, multiplicity, base = {}, [], 0
    for m in MULTIPLICITIES:
        mine = [x[1:] for x in pixels if x[0] == m]
        for n, x in enumerate(mine):
            place[x] = (n % CHUNKS, base + n // CHUNKS)
        rows = -(-len(mine) // CHUNKS)
        multiplicity += [m] * rows
        base += rows
    return place, multiplicity


WINDOW, MULTIPLICITY = window()
KROWS = len(MULTIPLICITY)

_at = 0


def _columns(n):
    global _at
    _at += n
    return slice(_at - n, _at)


C_IDENT = _columns(128)
C_IOTA = _columns(128)
C_BEFORE = _columns(128)
C_HEADS = _columns(HG)
C_FIRST = _columns(EXPERTS)
C_PAIR = _columns(PAIRS)
C_MEAN = _columns(1)
C_VALID = _columns(1)
C_JUNK = _columns(1)
C_TOKEN = _columns(1)
C_PICK = _columns(1)
C_POWER = _columns(1)
C_EPS = _columns(1)
C_WIDTH = _at


def at_least(eng, sem, value):
    if not isinstance(value, int) or value > 0:
        eng.wait_ge(sem, value)


def fixed_steps(i, count):
    def at(k):
        n = i + k
        return Step(n, n // 2, n % 2, n // 4, n % 4) if 0 <= n < count else None
    return at


def moving_steps(j, u):
    def at(k):
        c = 5 + u + k
        return Step(j * 4 + c, j * 2 + c // 2, c % 2, j + c // 4, c % 4)
    return at


def blocks_loop(eng, body):
    trips = (BLOCKS - 8) // 4
    for i in range(-3, 5):
        body(fixed_steps(i, BLOCKS))
    with eng.Fori(0, trips) as j:
        for u in range(4):
            body(moving_steps(j, u))
    for i in range(5 + 4 * trips, BLOCKS - 1):
        body(fixed_steps(i, BLOCKS))


def pairs_loop(eng, body, block_body, blocks_first=False):
    for i in range(-1, 5):
        steps = [(body, fixed_steps(i, PAIRS))]
        if 0 <= i < 4:
            steps.insert(0 if blocks_first else 1, (block_body, fixed_steps(BLOCKS - 1 + i, BLOCKS)))
        for step, at in steps:
            step(at)
    with eng.Fori(0, (PAIRS - 8) // 4) as j:
        for u in range(4):
            body(moving_steps(j, u))
    for i in range(PAIRS - 3, PAIRS + 3):
        body(fixed_steps(i, PAIRS))


def tiles_loop(eng, body):
    for i in range(-2, 5):
        body(fixed_steps(i, TILES))
    with eng.Fori(0, (TILES - 8) // 4) as j:
        for u in range(4):
            body(moving_steps(j, u))
    for i in range(TILES - 3, TILES + 1):
        body(fixed_steps(i, TILES))


def build(nc, consts, xcol, wtok, gamma, beta, tok_b, wqkv, wproj, wrouter, w1, w2, b2, out):
    assert PAIRS % 4 == 0 and TILES % 4 == 0
    with ExitStack() as ctx:
        def sb(name, shape, dt=F32):
            return ctx.enter_context(nc.sbuf_tensor(name, shape, dt))

        def bank(name):
            return ctx.enter_context(nc.psum_tensor(name, [128, 512], F32))

        def sem(name):
            return ctx.enter_context(nc.semaphore(name))

        h0_dram = nc.dram_tensor("token_h0", [TOKENS, DIM], F32, kind="Internal").ap()
        rows_dram = nc.dram_tensor("token_rows", [TOKENS, ROW], F32, kind="Internal").ap()
        out_rows = out.rearrange("b s d -> (b s) d")

        cst = sb("cst", [128, C_WIDTH])
        ident = cst[:, C_IDENT]
        gam = sb("gam", [KROWS, CHUNKS, SHIFTS])
        bet = sb("bet", [KROWS, CHUNKS, SHIFTS])
        tokb = sb("tokb", [1, DIM])
        ones = sb("ones", [128, 128])
        weff = sb("weff", [KROWS, CHUNKS, DIM + 1])
        c1 = sb("c1", [128, DIM])
        c0 = sb("c0", [128, DIM])
        wqkv_sb = sb("wqkv_sb", [HALF + 1, 2, 3 * DIM])
        wproj_sb = sb("wproj_sb", [HALF + 1, 2, DIM])
        wrouter_sb = sb("wrouter_sb", [HALF + 1, 2, EXPERTS])
        w2_sb = sb("w2_sb", [128, EXPERTS, FT, DIM])
        wt_in = w2_sb[0:KROWS].rearrange("k e f d -> k (e f) d")[:, 0:CHUNKS * SHIFTS, :]\
            .rearrange("k (c s) d -> k c s d", c=CHUNKS)
        b2_sb = sb("b2_sb", [128, EXPERTS, DIM])

        x_mem = sb("x_mem", [128, 4, CHUNKS * 128])
        xt = [x_mem[0:KROWS, i].rearrange("k (c t) -> k c t", c=CHUNKS) for i in range(4)]
        sq = [sb(f"sq{i}", [KROWS, CHUNKS, 128]) for i in range(2)]
        sqr = [sb(f"sqr{i}", [KROWS, 128]) for i in range(2)]
        c0_half = sb("c0_half", [128, DIM])
        tok_st = sb("tok_st", [128, 2])
        tok_m2 = sb("tok_m2", [128, 1])
        tok_var = sb("tok_var", [128, 1])
        tok_rs = sb("tok_rs", [128, 1])
        hb = [sb(f"hb{i}", [128, DIM]) for i in range(2)]
        bn1, mv1, ve1, rs1 = (sb(n, [128, k]) for n, k in (("bn1", 6), ("mv1", 2), ("ve1", 1), ("rs1", 1)))
        bn2, mv2, ve2, rs2 = (sb(n, [128, k]) for n, k in (("bn2", 6), ("mv2", 2), ("ve2", 1), ("rs2", 1)))
        xn = [sb(f"xn{i}", [128, DIM]) for i in range(2)]
        xnT = sb("xnT", [HALF, 2, BLOCKS * 128])
        xp = [sb(f"xp{i}", [HALF + 1, 2, SPAN]) for i in range(2)]
        h0 = [sb(f"h0_{i}", [128, DIM]) for i in range(4)]
        qk = [sb(f"qk{i}", [HALF, 2 * GROUPS, SPAN]) for i in range(2)]
        km = sb("km", [HALF, GROUPS, 2, HG, SEQ])
        vb = [sb(f"vb{i}", [128, 2, HG, 2 * (DH + 1)]) for i in range(2)]
        ss = sb("ss", [128, GROUPS, HG, SEQ])
        smx = sb("smx", [128, GROUPS, HG])
        pr = sb("pr", [128, HEADS, SLOT])
        prT = sb("prT", [128, HG, 128])
        rden = sb("rden", [128, HG, 2])
        o = sb("o", [128, DIM])
        oT = sb("oT", [HALF + 1, 2, 128])
        row = [sb(f"row{i}", [128, ROW]) for i in range(2)]
        x2T = sb("x2T", [HALF + 1, 2, 128])
        logits = sb("logits", [128, PAIRS, EXPERTS])

        qk_ps, v_ps, s0_ps, s1_ps, o_ps, t2_ps, t3_ps, lg_ps = (
            bank(n) for n in ("qk_ps", "v_ps", "s0_ps", "s1_ps", "o_ps", "t2_ps", "t3_ps", "lg_ps"))
        s_ps = (s0_ps, s1_ps)
        y_ps, t1_ps, c1_ps, c0_ps = (t2_ps, o_ps, v_ps, lg_ps), t3_ps, s0_ps, s1_ps

        r_mx = sb("r_mx", [128, PAIRS])
        r_sh = sb("r_sh", [128, PAIRS, EXPERTS])
        r_ex = sb("r_ex", [128, PAIRS, EXPERTS])
        r_den = sb("r_den", [128, PAIRS])
        r_prob = sb("r_prob", [128, PAIRS])
        r_eq = sb("r_eq", [128, PAIRS, EXPERTS])
        r_w = sb("r_w", [128, PAIRS, EXPERTS])
        r_wm = sb("r_wm", [128, PAIRS])
        r_ohb = sb("r_ohb", [128, PAIRS, EXPERTS], BF16)
        before_b = sb("before_b", [128, 128], BF16)
        valid_b = sb("valid_b", [128, 128], BF16)
        iota_b = sb("iota_b", [128, 128], BF16)
        one1 = sb("one1", [128, EXPERTS * PAIRS])
        r_tot = sb("r_tot", [128, EXPERTS, PAIRS])
        r_cum = sb("r_cum", [128, EXPERTS, PAIRS])
        r_prev = sb("r_prev", [128, EXPERTS])
        r_cnt = sb("r_cnt", [128, EXPERTS], I32)
        r_nti = sb("r_nti", [128, EXPERTS], I32)
        r_nt = sb("r_nt", [128, EXPERTS])
        r_end = sb("r_end", [128, EXPERTS])
        r_start = sb("r_start", [128, EXPERTS])
        r_base = sb("r_base", [128, EXPERTS])
        r_off2 = sb("r_off2", [128, EXPERTS, PAIRS])
        r_off3 = sb("r_off3", [128, PAIRS, EXPERTS])
        r_pos4 = sb("r_pos4", [128, PAIRS, EXPERTS])
        r_posf = sb("r_posf", [128, PAIRS])
        r_pos = sb("r_pos", [128, PAIRS], I32)
        r_modi = sb("r_modi", [128, PAIRS], I32)
        r_divi = sb("r_divi", [128, PAIRS], I32)
        r_mod = sb("r_mod", [128, PAIRS], BF16)
        r_div = sb("r_div", [128, PAIRS], BF16)
        r_ends = sb("r_ends", [128, TILES, EXPERTS])
        r_eidf = sb("r_eidf", [128, TILES])
        eid = sb("eid", [128, TILES], I32)
        vals = sb("vals", [128, PAIRS, VALUES], BF16)
        r_res = sb("r_res", [128, PAIRS])
        r_res2 = sb("r_res2", [128, PAIRS])
        slot_oh = sb("slot_oh", [128, PAIRS, 128], BF16)
        tile_oh = sb("tile_oh", [128, PAIRS, TILES], BF16)
        tile_v = sb("tile_v", [128, PAIRS, VALUES, TILES], BF16)
        got = sb("got", [128, VALUES, TILES])
        g_idx = sb("g_idx", [128, TILES])
        g_empty = sb("g_empty", [128, TILES])
        g_p12 = sb("g_p12", [128, TILES])
        prob = sb("prob", [128, TILES])
        gather_at = sb("gather_at", [128, TILES], U32)
        scatter_at = sb("scatter_at", [128, TILES], U32)

        w1s = [x_mem[0:HALF + 1, 2 * i:2 * i + 2].rearrange("k a f -> k (a f)")[:, 0:2 * FFN]
               .rearrange("k (a f) -> k a f", a=2) for i in range(2)]
        g = [sb(f"g{i}", [128, ROW]) for i in range(4)]
        gT = sb("gT", [HALF + 1, 2, 128])
        hT = [sb(f"hT{i}", [128, FT, TILE]) for i in range(2)]
        yb = sb("yb", [128, DIM])
        g_at = [sb(f"g_at{i}", [128, 1], U32) for i in range(4)]
        s_at = [sb(f"s_at{i}", [128, 1], U32) for i in range(2)]
        res = [sb(f"res{i}", [128, DIM]) for i in range(2)]

        consts_in, gb_in, wq_in, w2_in = sem("consts_in"), sem("gb_in"), sem("wq_in"), sem("w2_in")
        wt_in_sem = [sem(f"wt_in{c}") for c in range(CHUNKS)]
        h0_zero = sem("h0_zero")
        init_done = sem("init_done")
        weff_first, weff_step = sem("weff_first"), sem("weff_step")
        c1_mm, c1_sb, centred = sem("c1_mm"), sem("c1_sb"), sem("centred")
        c0_half_mm, c0_half_sb, c0_mm, c0_sb = sem("c0_half_mm"), sem("c0_half_sb"), sem("c0_mm"), sem("c0_sb")
        x_in = [sem(f"x_in{i}") for i in range(4)]
        hb_out = [sem(f"hb_out{i}") for i in range(2)]
        h0_in = [sem(f"h0_in{i}") for i in range(4)]
        xp_done = sem("xp_done")
        sq_done, sqr_done, tok_mm = sem("sq_done"), sem("sqr_done"), sem("tok_mm")
        st_done, m2_done, var_done, tok_rstd, hb_done = (
            sem("st_done"), sem("m2_done"), sem("var_done"), sem("tok_rstd"), sem("hb_done"))
        bn1_done, mv1_done, ve1_done, rs1_done, xn_done = (
            sem("bn1_done"), sem("mv1_done"), sem("ve1_done"), sem("rs1_done"), sem("xn_done"))
        t1_mm, xnT_done, qk_mm, v_mm, qk_sb, km_done, v_sb = (
            sem("t1_mm"), sem("xnT_done"), sem("qk_mm"), sem("v_mm"), sem("qk_sb"), sem("km_done"), sem("v_sb"))
        s_mm, smax, ssub, p_done, pt_mm, pt_sb = (
            sem("s_mm"), sem("smax"), sem("ssub"), sem("p_done"), sem("pt_mm"), sem("pt_sb"))
        pv_mm, rden_done, o_done, t2_mm, oT_done, pj_mm = (
            sem("pv_mm"), sem("rden_done"), sem("o_done"), sem("t2_mm"), sem("oT_done"), sem("pj_mm"))
        h1_done, bn2_done, mv2_done, ve2_done, rs2_done, xn2_done = (
            sem("h1_done"), sem("bn2_done"), sem("mv2_done"), sem("ve2_done"), sem("rs2_done"), sem("xn2_done"))
        row_out = [sem(f"row_out{i}") for i in range(2)]
        t3_mm, x2T_done, lg_mm, lg_done = sem("t3_mm"), sem("x2T_done"), sem("lg_mm"), sem("lg_done")
        r_step = sem("r_step")
        r_exp, r_counts, r_sb = sem("r_exp"), sem("r_counts"), sem("r_sb")
        places_done, slots_ready = sem("places_done"), sem("slots_ready")
        index_ready, index_placed = sem("index_ready"), sem("index_placed")
        prob_ready, prob_placed, prob_read = sem("prob_ready"), sem("prob_placed"), sem("prob_read")
        eid_done, idx_done = sem("eid_done"), sem("idx_done")
        w1_in = [sem(f"w1_in{i}") for i in range(2)]
        g_in = [sem(f"g_in{i}") for i in range(4)]
        gt_mm, gT_done, up_mm, gelu_done, down_mm = (
            sem("gt_mm"), sem("gT_done"), sem("up_mm"), sem("gelu_done"), sem("down_mm"))
        yb_done, res_done = sem("yb_done"), sem("res_done")
        g_at_done, s_at_done = sem("g_at_done"), sem("s_at_done")
        res_out = [sem(f"res_out{i}") for i in range(2)]

        waited = [sem("waited_dve"), sem("waited_pool")]

        def apart(eng):
            eng.sem_inc(waited[0 if eng is nc.vector else 1], 1)

        def tile_values(eng, values, ready):
            for n in range(0, PAIRS, 8):
                for v in range(values.start, values.stop):
                    ins = eng.tensor_tensor(tile_v[:, n:n + 8, v, :], tile_oh[:, n:n + 8, :],
                                            vals[:, n:n + 8, v].unsqueeze(2).to_broadcast([128, 8, TILES]), ALU.mult)
                ins.then_inc(ready, 1)

        block = ctx.enter_context(nc.Block())

        @block.sync
        def _(sp):
            for c in range(CHUNKS):
                sp.dma_start(wt_in[:, c], wtok[:, c]).then_inc(wt_in_sem[c], 16)

            def load_x(b):
                at_least(sp, tok_mm, b.n - 3)
                at_least(sp, sq_done, b.n - 3)
                src = xcol[bass.ds(b.n, 1)].rearrange("a k c t -> (a k) c t")
                sp.dma_start(xt[b.ring][:], src).then_inc(x_in[b.ring], 16)

            def store_embedding(b):
                sp.wait_ge(hb_done, b.n + 1)
                rows = LAST_ROWS if isinstance(b.n, int) and b.n == BLOCKS - 1 else 128
                sp.dma_start(h0_dram[bass.ds(b.n * 128, rows), :], hb[b.par][0:rows, :]).then_inc(hb_out[b.par], 16)

            def block_body(block):
                if b := block(3):
                    load_x(b)
                if b := block(-1):
                    store_embedding(b)

            blocks_loop(sp, block_body)

            def load_second_layer(p):
                if isinstance(p.n, int) and p.n == 0:
                    sp.wait_ge(c0_half_mm, 1)
                    sp.wait_ge(centred, CHUNKS)
                    sp.dma_start(b2_sb[:], b2.unsqueeze(0).to_broadcast([128, EXPERTS, DIM])).then_inc(w2_in, 16)
                width = EXPERTS * FT * DIM // PAIRS
                part = bass.ds(p.n * width, width)
                sp.dma_start(w2_sb[:].rearrange("k e f d -> k (e f d)")[:, part],
                             w2.rearrange("k e f d -> k (e f d)")[:, part]).then_inc(w2_in, 16)

            def load_embedding(p):
                if isinstance(p.n, int) and p.n == 0:
                    for i in range(2):
                        sp.wait_ge(hb_out[i], 16 * ((BLOCKS + 1 - i) // 2))
                at_least(sp, h1_done, p.n - 3)
                for a in range(2):
                    sp.dma_start(h0[p.ring][a * SLOT:a * SLOT + SEQ, :],
                                 h0_dram[bass.ds(p.n * PAIR_TOKENS + a * SEQ, SEQ), :]).then_inc(h0_in[p.ring], 16)

            def store_rows(p):
                sp.wait_ge(xn2_done, p.n + 1)
                for a in range(2):
                    sp.dma_start(rows_dram[bass.ds(p.n * PAIR_TOKENS + a * SEQ, SEQ), :],
                                 row[p.par][a * SLOT:a * SLOT + SEQ, :]).then_inc(row_out[p.par], 16)

            def body(pair):
                if p := pair(-1):
                    load_embedding(p)
                if p := pair(0):
                    load_second_layer(p)
                if p := pair(-3):
                    store_rows(p)

            pairs_loop(sp, body, block_body, blocks_first=True)

            sp.wait_ge(eid_done, 1)

            def tile_body(tile):
                if t := tile(2):
                    at_least(sp, up_mm, 2 * (t.n - 1))
                    e = sp.value_load(eid[0:1, bass.ds(t.n, 1)], min_val=0, max_val=EXPERTS - 1)
                    sp.dma_start(w1s[t.par][:], w1[bass.ds(e, 1)].rearrange("e k c f -> (e k) c f"))\
                        .then_inc(w1_in[t.par], 16)

            tiles_loop(sp, tile_body)
            for i in range(2):
                sp.wait_ge(row_out[i], 32 * (PAIRS // 2))
                sp.wait_ge(res_out[i], 16 * (TILES // 2))

        @block.tensor
        def _(pe):
            def sum_beta(first):
                for s in range(SHIFTS):
                    for i in range(2):
                        c = first + i
                        if s == 0:
                            pe.wait_ge(wt_in_sem[c], 16)
                        mm = pe.matmul(c0_ps[i * 64:(i + 1) * 64, 0:DIM],
                                       bet[:, c, s:s + 1].to_broadcast([KROWS, 64]), wt_in[:, c, s, :],
                                       start=(first == 0 and s == 0), stop=(first == CHUNKS - 2 and s == SHIFTS - 1))
                return mm

            pe.wait_ge(init_done, 1)
            pe.wait_ge(gb_in, 16 * 3)
            sum_beta(0)
            for c in range(CHUNKS):
                if c % 2 == 0 and c + 2 < CHUNKS:
                    last = sum_beta(c + 2)
                    if c + 4 == CHUNKS:
                        last.then_inc(c0_half_mm, 1)
                pe.wait_ge(weff_step, 2 * (SHIFTS - 1) * (c // 2 + 1) - 1 + c % 2)
                mm = pe.matmul(c1_ps[:, 0:DIM], ones[0:KROWS, :], weff[:, c, 0:DIM],
                               start=(c == 0), stop=(c == CHUNKS - 1))
            mm.then_inc(c1_mm, 1)

            def fold_beta():
                pe.wait_ge(c0_half_sb, 1)
                pe.wait_ge(consts_in, 16)
                pe.matmul(c0_ps[:, 256:256 + DIM], cst[:, C_PICK].to_broadcast([128, 128]), c0_half[:, :],
                          start=True, stop=False)
                pe.matmul(c0_ps[:, 256:256 + DIM], ones[0:1, :], tokb[:, :], start=False, stop=True).then_inc(c0_mm, 1)

            def tokens(b):
                pe.wait_ge(x_in[b.ring], 16 * (b.quad + 1))
                at_least(pe, hb_done, b.n - 3)
                y = y_ps[b.ring]
                for c in range(CHUNKS):
                    if isinstance(b.n, int) and b.n == 0:
                        pe.wait_ge(centred, c + 1)
                    pe.matmul(y[:, 0:DIM + 1], xt[b.ring][:, c, :], weff[:, c, :],
                              start=(c == 0), stop=(c == CHUNKS - 1))
                pe.wait_ge(sqr_done, b.n + 1)
                pe.matmul(y[:, DIM + 1:DIM + 2], sqr[b.par][:, :], cst[0:KROWS, C_MEAN],
                          start=True, stop=True).then_inc(tok_mm, 1)

            def turn(src, dst, n, ready, done):
                pe.wait_ge(ready, n + 1)
                for k in range(2):
                    mm = pe.transpose(dst[0:HALF, k * 128:(k + 1) * 128],
                                      src[:, k * HALF:(k + 1) * HALF], ident)
                mm.then_inc(done, 1)

            def block_body(block):
                if b := block(0):
                    tokens(b)
                    if isinstance(b.n, int) and b.n == 0:
                        fold_beta()
                if b := block(-3):
                    at_least(pe, xnT_done, b.n)
                    if isinstance(b.n, int) and b.n == BLOCKS - 1:
                        pe.wait_ge(x2T_done, 1)
                    turn(xn[b.par], t1_ps, b.n, xn_done, t1_mm)

            blocks_loop(pe, block_body)

            def project_qk(p):
                pe.wait_ge(xp_done, p.n + 1)
                at_least(pe, qk_sb, p.n)
                for m in range(2 * GROUPS):
                    for k in range(2):
                        kr = HALF + 1 - k
                        mm = pe.matmul(qk_ps[0:HALF, m * PAIR_TOKENS:(m + 1) * PAIR_TOKENS],
                                       wqkv_sb[0:kr, k, m * HALF:(m + 1) * HALF], xp[p.par][0:kr, k, 0:PAIR_TOKENS],
                                       start=(k == 0), stop=(k == 1))
                mm.then_inc(qk_mm, 1)

            def project_v(p):
                if isinstance(p.n, int) and p.n == 0:
                    pe.wait_ge(hb_done, BLOCKS - 2)
                at_least(pe, v_sb, p.n)
                for odd in range(2):
                    w = slice(2 * DIM + odd * HALF, 2 * DIM + (odd + 1) * HALF)
                    for a in range(2):
                        for k in range(2):
                            kr = HALF + 1 - k
                            mm = pe.matmul(v_ps[odd * SLOT:(odd + 1) * SLOT, a * HALF:(a + 1) * HALF],
                                           xp[p.par][0:kr, k, a * SEQ:a * SEQ + SLOT], wqkv_sb[0:kr, k, w],
                                           start=(k == 0), stop=(k == 1))
                mm.then_inc(v_mm, 1)

            def scores(p):
                pe.wait_ge(km_done, p.n + 1)
                for gr in range(GROUPS):
                    at_least(pe, pt_sb, 2 * p.n - 1 + gr)
                    for a in range(2):
                        mm = pe.matmul(s_ps[gr][a * SLOT:(a + 1) * SLOT, 0:HG * SEQ],
                                       qk[p.par][:, 2 * gr, a * SEQ:a * SEQ + SLOT],
                                       km[:, gr, a].rearrange("k h t -> k (h t)"), start=True, stop=True)
                    mm.then_inc(s_mm, 1)

            def turn_probs(p):
                for gr in range(GROUPS):
                    pe.wait_ge(p_done, 2 * p.n + 1 + gr)
                    for i in range(HG // 2):
                        hp = gr * (HG // 2) + i
                        mm = pe.transpose(s_ps[gr][:, i * 128:(i + 1) * 128],
                                          pr[:, 2 * hp:2 * hp + 2, :].rearrange("p h t -> p (h t)"), ident)
                    mm.then_inc(pt_mm, 1)

            def mix(p):
                pe.wait_ge(v_sb, p.n + 1)
                at_least(pe, h1_done, p.n)
                for hp in range(HG):
                    if hp % (HG // 2) == 0:
                        pe.wait_ge(pt_sb, 2 * p.n + 1 + hp // (HG // 2))
                    for a in range(2):
                        mm = pe.matmul(o_ps[a * SLOT:(a + 1) * SLOT, hp * 34:(hp + 1) * 34],
                                       prT[:, hp, a * SLOT:(a + 1) * SLOT], vb[p.par][:, a, hp, :],
                                       start=True, stop=True)
                mm.then_inc(pv_mm, 1)

            def project(p):
                pe.wait_ge(oT_done, p.n + 1)
                for k in range(2):
                    kr = HALF + 1 - k
                    mm = pe.matmul(o_ps[:, 0:DIM], oT[0:kr, k, :], wproj_sb[0:kr, k, :],
                                   start=(k == 0), stop=(k == 1))
                mm.then_inc(pj_mm, 1)

            def router(p):
                pe.wait_ge(x2T_done, p.n + 1)
                at_least(pe, lg_done, p.n)
                for k in range(2):
                    kr = HALF + 1 - k
                    mm = pe.matmul(lg_ps[:, 0:EXPERTS], x2T[0:kr, k, :], wrouter_sb[0:kr, k, :],
                                   start=(k == 0), stop=(k == 1))
                mm.then_inc(lg_mm, 1)

            def body(pair):
                if p := pair(0):
                    if isinstance(p.n, int) and p.n == 0:
                        pe.wait_ge(wq_in, 16 * 3)
                    project_qk(p)
                if p := pair(-2):
                    if isinstance(p.n, int) and p.n == 0:
                        pe.wait_ge(hb_done, BLOCKS)
                    at_least(pe, oT_done, p.n)
                    turn(o, t2_ps, p.n, o_done, t2_mm)
                if p := pair(-1):
                    scores(p)
                if p := pair(-2):
                    project(p)
                if p := pair(-3):
                    if isinstance(p.n, int) and p.n < 2:
                        pe.wait_ge(xnT_done, BLOCKS - 1 + p.n)
                    at_least(pe, x2T_done, p.n)
                    turn(row[p.par], t3_ps, p.n, xn2_done, t3_mm)
                if p := pair(0):
                    project_v(p)
                if p := pair(-1):
                    turn_probs(p)
                if p := pair(-3):
                    router(p)
                if p := pair(-1):
                    mix(p)

            pairs_loop(pe, body, block_body)

            pe.wait_ge(r_counts, 1)
            flat = r_ohb[:].rearrange("p a e -> p (a e)")
            pe.matmul(s_ps[0][:, 0:PAIRS * EXPERTS], before_b[:, :], flat, start=True, stop=True)
            pe.matmul(s_ps[1][:, 0:PAIRS * EXPERTS], valid_b[:, :], flat, start=True, stop=True)\
                .then_inc(r_sb, 1)

            def place(values, dst, ready, done):
                for n in range(PAIRS):
                    if n % 8 == 0:
                        pe.wait_ge(slots_ready, n // 8 + 1)
                        pe.wait_ge(ready, n // 8 + 1)
                    mm = pe.matmul(dst[:, 0:TILES * (values.stop - values.start)], slot_oh[:, n, :],
                                   tile_v[:, n, values, :].rearrange("p v t -> p (v t)"),
                                   start=(n == 0), stop=(n == PAIRS - 1))
                mm.then_inc(done, 1)

            place(INDEX, o_ps, index_ready, index_placed)

            h_ps = ((s0_ps, s1_ps), (qk_ps, v_ps))
            out_ps = (lg_ps, t2_ps)
            pe.wait_ge(w2_in, 16 * (PAIRS + 1))

            def turn_rows(t):
                pe.wait_ge(g_in[t.ring], 16 * (t.quad + 1))
                at_least(pe, gT_done, t.n)
                for k in range(2):
                    mm = pe.transpose(t3_ps[0:HALF, k * 128:(k + 1) * 128],
                                      g[t.ring][:, k * HALF:(k + 1) * HALF], ident)
                mm.then_inc(gt_mm, 1)

            def up(t):
                pe.wait_ge(gT_done, t.n + 1)
                if isinstance(t.n, int) and t.n == 1:
                    pe.wait_ge(prob_read, 1)
                pe.wait_ge(w1_in[t.par], 16 * (t.half + 1))
                for hb in range(2):
                    at_least(pe, gelu_done, 2 * (t.n - 2) + 1 + hb)
                    for i in range(FH):
                        f = hb * FH + i
                        for k in range(2):
                            kr = HALF + 1 - k
                            mm = pe.matmul(h_ps[t.par][hb][:, i * TILE:(i + 1) * TILE],
                                           w1s[t.par][0:kr, k, f * 128:(f + 1) * 128], gT[0:kr, k, :],
                                           start=(k == 0), stop=(k == 1))
                    mm.then_inc(up_mm, 1)

            def down(t):
                e = pe.value_load(eid[0:1, bass.ds(t.n, 1)], min_val=0, max_val=EXPERTS - 1)
                at_least(pe, yb_done, t.n - 1)
                for f in range(FT):
                    if f % FH == 0:
                        pe.wait_ge(gelu_done, 2 * t.n + 1 + f // FH)
                    mm = pe.matmul(out_ps[t.par][:, 0:DIM], hT[t.par][:, f, :],
                                   w2_sb[:, bass.ds(e, 1), f, :].rearrange("p e d -> p (e d)"),
                                   start=(f == 0), stop=(f == FT - 1))
                mm.then_inc(down_mm, 1)

            def tile_body(tile):
                if t := tile(0):
                    up(t)
                    if isinstance(t.n, int) and t.n == 0:
                        place(PROB, v_ps, prob_ready, prob_placed)
                if t := tile(1):
                    turn_rows(t)
                if t := tile(-1):
                    down(t)

            pe.wait_ge(eid_done, 1)
            tiles_loop(pe, tile_body)

        @block.scalar
        def _(act):
            act.dma_start(cst[:], consts).then_inc(consts_in, 16)
            act.dma_start(gam[:], gamma).then_inc(gb_in, 16)
            act.dma_start(bet[:], beta).then_inc(gb_in, 16)
            act.dma_start(tokb[:], tok_b.rearrange("(a d) -> a d", a=1)).then_inc(gb_in, 16)
            act.wait_ge(gb_in, 16 * 3)
            for c in range(CHUNKS):
                act.wait_ge(wt_in_sem[c], 16)
                act.activation(weff[:, c, 0:DIM], wt_in[:, c, 0, :], ACT.Copy, scale=gam[:, c, 0:1])\
                    .then_inc(weff_first, 1)
            act.wait_ge(c0_half_mm, 1)
            act.copy(c0_half[:], c0_ps[:, 0:DIM]).then_inc(c0_half_sb, 1)
            act.dma_start(wqkv_sb[:], wqkv).then_inc(wq_in, 16)
            act.dma_start(wproj_sb[:], wproj).then_inc(wq_in, 16)
            act.dma_start(wrouter_sb[:], wrouter).then_inc(wq_in, 16)

            def square(b):
                act.wait_ge(x_in[b.ring], 16 * (b.quad + 1))
                at_least(act, sqr_done, b.n - 1)
                act.activation(sq[b.par][:], xt[b.ring][:], ACT.Square).then_inc(sq_done, 1)

            def copy_block(b):
                act.wait_ge(t1_mm, b.n + 1)
                act.copy(xnT[:, :, bass.ds(b.n * 128, 128)],
                         t1_ps[0:HALF, 0:256].rearrange("k (a t) -> k a t", a=2)).then_inc(xnT_done, 1)

            def copy_pair(p):
                act.wait_ge(xnT_done, min(BLOCKS, (p.n * PAIR_TOKENS + SPAN - 1) // 128 + 1)
                            if isinstance(p.n, int) else BLOCKS)
                at_least(act, v_mm, p.n - 1)
                act.copy(xp[p.par][0:HALF, :, :], xnT[:, :, bass.ds(p.n * PAIR_TOKENS, SPAN)]).then_inc(xp_done, 1)

            def copy_turned(dst, src, ready, used, n, done):
                act.wait_ge(ready, n + 1)
                at_least(act, used, n)
                act.copy(dst[0:HALF, :, :].rearrange("k a t -> k (a t)"), src[0:HALF, 0:256]).then_inc(done, 1)

            def exps(p, gr):
                act.wait_ge(ssub, 2 * p.n + 1 + gr)
                at_least(act, pt_mm, 2 * p.n - 1 + gr)
                act.activation(pr[:, gr * HG:(gr + 1) * HG, 0:SEQ], ss[:, gr], ACT.Exp,
                               scale=float(DH) ** -0.5).then_inc(p_done, 1)

            def copy_qk(p):
                act.wait_ge(qk_mm, p.n + 1)
                at_least(act, s_mm, 2 * p.n - 2)
                at_least(act, km_done, p.n - 1)
                act.copy(qk[p.par][:, :, 0:PAIR_TOKENS],
                         qk_ps[0:HALF, 0:4 * PAIR_TOKENS].rearrange("k (m t) -> k m t", m=4)).then_inc(qk_sb, 1)

            def copy_probs(p):
                at_least(act, pv_mm, p.n)
                for gr in range(GROUPS):
                    act.wait_ge(pt_mm, 2 * p.n + 1 + gr)
                    act.copy(prT[:, gr * 3:gr * 3 + 3, :].rearrange("p h s -> p (h s)"),
                             s_ps[gr][:, 0:384]).then_inc(pt_sb, 1)

            act.wait_ge(init_done, 1)

            def block_body(block):
                if b := block(2):
                    square(b)
                if b := block(-3):
                    copy_block(b)

            blocks_loop(act, block_body)

            def body(pair):
                if p := pair(0):
                    copy_qk(p)
                if p := pair(-2):
                    copy_turned(oT, t2_ps, t2_mm, pj_mm, p.n, oT_done)
                if p := pair(-1):
                    exps(p, 0)
                if p := pair(-3):
                    copy_turned(x2T, t3_ps, t3_mm, lg_mm, p.n, x2T_done)
                if p := pair(-1):
                    exps(p, 1)
                    copy_probs(p)
                if p := pair(1):
                    copy_pair(p)

            pairs_loop(act, body, block_body)

            act.wait_ge(r_exp, 1)
            act.activation(r_ex[:], r_sh[:], ACT.Exp).then_inc(r_exp, 1)

            def gelus(t):
                h_ps = ((s0_ps, s1_ps), (qk_ps, v_ps))
                at_least(act, down_mm, t.n - 1)
                for hb in range(2):
                    act.wait_ge(up_mm, 2 * t.n + 1 + hb)
                    act.activation(hT[t.par][:, hb * FH:(hb + 1) * FH, :].rearrange("p f t -> p (f t)"),
                                   h_ps[t.par][hb][:, 0:FH * TILE], ACT.Gelu).then_inc(gelu_done, 1)

            def copy_rows(t):
                act.wait_ge(gt_mm, t.n + 1)
                at_least(act, up_mm, 2 * t.n)
                act.copy(gT[0:HALF, :, :].rearrange("k a t -> k (a t)"), t3_ps[0:HALF, 0:256]).then_inc(gT_done, 1)

            def tile_body(tile):
                if t := tile(0):
                    gelus(t)
                if t := tile(1):
                    copy_rows(t)

            tiles_loop(act, tile_body)

        @block.gpsimd
        def _(pool):
            for x in h0:
                x_zero = pool.memset(x[:], 0.0)
            x_zero.then_inc(h0_zero, 1)
            pool.wait_ge(init_done, 1)
            pool.wait_ge(consts_in, 16)

            def mask_k(p):
                pool.wait_ge(qk_sb, p.n + 1)
                at_least(pool, s_mm, 2 * p.n)
                heads = cst[0:HALF, C_HEADS].unsqueeze(2).to_broadcast([HALF, HG, SEQ])
                for gr in range(GROUPS):
                    for a in range(2):
                        k = qk[p.par][:, 2 * gr + 1, a * SEQ:(a + 1) * SEQ].unsqueeze(1).to_broadcast([HALF, HG, SEQ])
                        last = pool.tensor_tensor(km[:, gr, a], k, heads, ALU.mult)
                last.then_inc(km_done, 1)

            def inverse_deviation(mv, ve, rs, n, ready, ve_sem, done):
                pool.wait_ge(ready, n + 1)
                pool.tensor_tensor(ve[:], mv[:, 1:2], cst[:, C_EPS], ALU.add).then_inc(ve_sem, 1)
                pool.wait_ge(ve_sem, n + 1)
                pool.tensor_tensor(rs[:], ve[:], cst[:, C_POWER], ALU.pow).then_inc(done, 1)

            def token_deviation(p):
                pool.wait_ge(st_done, p.n + 1)
                pool.tensor_tensor(tok_m2[:], tok_st[:, 0:1], tok_st[:, 0:1], ALU.mult).then_inc(m2_done, 1)
                pool.wait_ge(m2_done, p.n + 1)
                pool.tensor_tensor(tok_var[:], tok_st[:, 1:2], tok_m2[:], ALU.subtract).then_inc(var_done, 1)
                pool.wait_ge(var_done, p.n + 1)
                pool.tensor_tensor(tok_rs[:], tok_var[:], cst[:, C_POWER], ALU.pow).then_inc(tok_rstd, 1)

            def block_body(block):
                if b := block(-1):
                    token_deviation(b)
                    inverse_deviation(mv1, ve1, rs1, b.n, mv1_done, ve1_done, rs1_done)

            blocks_loop(pool, block_body)

            def body(pair):
                if p := pair(0):
                    mask_k(p)
                if p := pair(-2):
                    inverse_deviation(mv2, ve2, rs2, p.n, mv2_done, ve2_done, rs2_done)

            pairs_loop(pool, body, block_body)

            pool.wait_ge(places_done, 1)
            tile_values(pool, INDEX, index_ready)

            pool.wait_ge(idx_done, 1)
            for i in range(2):
                pool.wait_ge(row_out[i], 32 * (PAIRS // 2))

            def gather(t):
                at_least(pool, res_done, t.n - 3)
                apart(pool)
                pool.tensor_copy(g_at[t.ring][:], gather_at[:, bass.ds(t.n, 1)]).then_inc(g_at_done, 1)
                pool.wait_ge(g_at_done, t.n + 1)
                apart(pool)
                pool.indirect_dma_start(g[t.ring][:, :], None, rows_dram[:, :],
                                        bass.IndirectOffsetOnAxis(ap=g_at[t.ring][:, 0:1], axis=0))\
                    .then_inc(g_in[t.ring], 16)

            def scatter(t):
                pool.wait_ge(res_done, t.n + 1)
                at_least(pool, res_out[t.par], t.half * 16)
                apart(pool)
                pool.tensor_copy(s_at[t.par][:], scatter_at[:, bass.ds(t.n, 1)]).then_inc(s_at_done, 1)
                pool.wait_ge(s_at_done, t.n + 1)
                apart(pool)
                pool.indirect_dma_start(out_rows, bass.IndirectOffsetOnAxis(ap=s_at[t.par][:, 0:1], axis=0),
                                        res[t.par][:, :], None, bounds_check=TOKENS - 1, oob_is_err=False)\
                    .then_inc(res_out[t.par], 16)

            def tile_body(tile):
                if t := tile(3):
                    gather(t)
                if t := tile(-1):
                    scatter(t)

            gather(Step(0, 0, 0, 0, 0))
            tiles_loop(pool, tile_body)

        @block.vector
        def _(dve):
            dve.memset(ones[:], 1.0)
            dve.memset(one1[:], 1.0)
            for x in (*xp, oT, x2T, gT):
                dve.memset(x[HALF:HALF + 1, :, :], 1.0)
            for x in qk:
                dve.memset(x[:, :, PAIR_TOKENS:SPAN], 0.0)
            dve.memset(pr[:, :, SEQ:SLOT], 0.0)
            dve.memset(r_prev[:, 0:1], 0.0)
            for v in vb:
                dve.memset(v[0:SLOT, :, :, DH + 1:2 * DH + 2], 0.0)
                dve.memset(v[SLOT:128, :, :, 0:DH + 1], 0.0)
                dve.memset(v[0:SLOT, :, :, DH:DH + 1], 1.0)
                last = dve.memset(v[SLOT:128, :, :, 2 * DH + 1:2 * DH + 2], 1.0)
            last.then_inc(init_done, 1)

            dve.wait_ge(gb_in, 16 * 3)
            step = 0
            for first in range(0, CHUNKS, 2):
                for s in range(1, SHIFTS):
                    for c in (first, first + 1):
                        if s == 1:
                            dve.wait_ge(weff_first, c + 1)
                        else:
                            dve.wait_ge(weff_step, step - 1)
                        dve.scalar_tensor_tensor(out=weff[:, c, 0:DIM], in0=wt_in[:, c, s, :],
                                                 scalar=gam[:, c, s:s + 1], in1=weff[:, c, 0:DIM],
                                                 op0=ALU.mult, op1=ALU.add).then_inc(weff_step, 1)
                        step += 1
            dve.wait_ge(consts_in, 16)
            for c in range(CHUNKS):
                dve.tensor_copy(weff[:, c, DIM:DIM + 1], cst[0:KROWS, C_MEAN])
            dve.wait_ge(c1_mm, 1)
            dve.tensor_scalar(c1[:], c1_ps[:, 0:DIM], cst[:, C_MEAN], None, ALU.mult).then_inc(c1_sb, 1)
            dve.wait_ge(c1_sb, 1)
            for c in range(CHUNKS):
                dve.tensor_tensor(weff[:, c, 0:DIM], weff[:, c, 0:DIM], c1[0:KROWS, :], ALU.subtract)\
                    .then_inc(centred, 1)
            dve.tensor_copy(valid_b[:], cst[:, C_VALID].to_broadcast([128, 128]))
            dve.tensor_copy(before_b[:], cst[:, C_BEFORE])
            dve.tensor_copy(iota_b[:], cst[:, C_IOTA])

            def normalise_mix(p):
                dve.wait_ge(pv_mm, p.n + 1)
                v = o_ps[:, 0:HEADS * (DH + 1)].rearrange("p (h d) -> p h d", h=HEADS)
                dve.reciprocal(rden[:].rearrange("p a b -> p (a b)"), v[:, :, DH]).then_inc(rden_done, 1)
                dve.wait_ge(rden_done, p.n + 1)
                at_least(dve, t2_mm, p.n)
                dve.tensor_tensor(o[:].rearrange("p (h d) -> p h d", h=HEADS), v[:, :, 0:DH],
                                  rden[:].rearrange("p a b -> p (a b)").unsqueeze(2).to_broadcast([128, HEADS, DH]),
                                  ALU.mult).then_inc(o_done, 1)

            def sum_squares(b):
                dve.wait_ge(sq_done, b.n + 1)
                at_least(dve, tok_mm, b.n - 1)
                dve.tensor_reduce(sqr[b.par][:, :], sq[b.par][:].rearrange("k c t -> k t c"), AX, ALU.add).then_inc(sqr_done, 1)

            def shift_scores(p):
                for gr in range(GROUPS):
                    dve.wait_ge(s_mm, 2 * p.n + 1 + gr)
                    v = s_ps[gr][:, 0:HG * SEQ].rearrange("p (h t) -> p h t", h=HG)
                    dve.tensor_reduce(smx[:, gr], v, AX, ALU.max).then_inc(smax, 1)
                    dve.wait_ge(smax, 2 * p.n + 1 + gr)
                    at_least(dve, p_done, 2 * p.n - 1 + gr)
                    dve.tensor_tensor(ss[:, gr], v, smx[:, gr].unsqueeze(2).to_broadcast([128, HG, SEQ]),
                                      ALU.subtract).then_inc(ssub, 1)

            def copy_logits(p):
                dve.wait_ge(lg_mm, p.n + 1)
                dve.tensor_copy(logits[:, bass.ds(p.n, 1), :].rearrange("p a e -> p (a e)"),
                                lg_ps[:, 0:EXPERTS]).then_inc(lg_done, 1)

            def copy_v(p):
                dve.wait_ge(v_mm, p.n + 1)
                at_least(dve, pv_mm, p.n - 1)
                v = v_ps[:, 0:DIM].rearrange("p (a h d) -> p a h d", a=2, h=HG)
                dve.tensor_copy(vb[p.par][0:SLOT, :, :, 0:DH], v[0:SLOT])
                dve.tensor_copy(vb[p.par][SLOT:128, :, :, DH + 1:2 * DH + 1], v[SLOT:128])\
                    .then_inc(v_sb, 1)

            def statistics(p, src, bn, mv, src_done, bn_sem, mv_sem):
                dve.wait_ge(src_done, p.n + 1)
                dve.bn_stats(bn[:], src).then_inc(bn_sem, 1)
                dve.wait_ge(bn_sem, p.n + 1)
                apart(dve)
                dve.bn_aggr(mv[:], bn[:]).then_inc(mv_sem, 1)

            def add_residual(p):
                dve.wait_ge(pj_mm, p.n + 1)
                dve.wait_ge(h0_in[p.ring], 32 * (p.quad + 1))
                at_least(dve, row_out[p.par], p.half * 32)
                at_least(dve, t3_mm, p.n - 1)
                dve.tensor_tensor(row[p.par][:, DIM:ROW], o_ps[:, 0:DIM], h0[p.ring][:], ALU.add).then_inc(h1_done, 1)
                statistics(p, row[p.par][:, DIM:ROW], bn2, mv2, h1_done, bn2_done, mv2_done)

            def second_norm(p):
                dve.wait_ge(mv2_done, p.n + 1)
                dve.wait_ge(rs2_done, p.n + 1)
                dve.tensor_scalar(row[p.par][:, 0:DIM], row[p.par][:, DIM:ROW], mv2[:, 0:1], rs2[:, 0:1],
                                  ALU.subtract, ALU.mult).then_inc(xn2_done, 1)

            def token_statistics(b):
                dve.wait_ge(tok_mm, b.n + 1)
                y = y_ps[b.ring]
                dve.tensor_copy(tok_st[:, 0:1], y[:, DIM:DIM + 1])
                dve.tensor_scalar(tok_st[:, 1:2], y[:, DIM + 1:DIM + 2], LN_EPS, None, ALU.add).then_inc(st_done, 1)

            def embed(b):
                if isinstance(b.n, int) and b.n == 0:
                    dve.wait_ge(c0_mm, 1)
                    dve.tensor_copy(c0[:], c0_ps[:, 256:256 + DIM]).then_inc(c0_sb, 1)
                    dve.wait_ge(c0_sb, 1)
                dve.wait_ge(tok_rstd, b.n + 1)
                at_least(dve, hb_out[b.par], b.half * 16)
                dve.scalar_tensor_tensor(out=hb[b.par][:], in0=y_ps[b.ring][:, 0:DIM], scalar=tok_rs[:, 0:1], in1=c0[:],
                                         op0=ALU.mult, op1=ALU.add).then_inc(hb_done, 1)
                statistics(b, hb[b.par][:], bn1, mv1, hb_done, bn1_done, mv1_done)

            def first_norm(b):
                dve.wait_ge(mv1_done, b.n + 1)
                at_least(dve, t1_mm, b.n - 1)
                dve.wait_ge(rs1_done, b.n + 1)
                dve.tensor_scalar(xn[b.par][:], hb[b.par][:], mv1[:, 0:1], rs1[:, 0:1],
                                  ALU.subtract, ALU.mult).then_inc(xn_done, 1)

            def block_body(block):
                if b := block(-1):
                    token_statistics(b)
                if b := block(1):
                    sum_squares(b)
                if b := block(-2):
                    first_norm(b)
                if b := block(-1):
                    embed(b)

            blocks_loop(dve, block_body)
            dve.wait_ge(h0_zero, 1)

            def body(pair):
                if p := pair(-2):
                    normalise_mix(p)
                if p := pair(-1):
                    shift_scores(p)
                if p := pair(-2):
                    add_residual(p)
                if p := pair(0):
                    copy_v(p)
                if p := pair(-2):
                    second_norm(p)
                if p := pair(-3):
                    copy_logits(p)

            pairs_loop(dve, body, block_body)

            done = [0]

            def step_(ins):
                done[0] += 1
                ins.then_inc(r_step, 1)
                dve.wait_ge(r_step, done[0])

            def over_experts(x):
                return x.unsqueeze(2).to_broadcast([128, PAIRS, EXPERTS])

            dve.wait_ge(lg_done, PAIRS)
            step_(dve.tensor_reduce(r_mx[:], logits[:], AX, ALU.max))
            dve.tensor_tensor(r_sh[:], logits[:], over_experts(r_mx[:]), ALU.subtract).then_inc(r_exp, 1)
            step_(dve.tensor_tensor(r_eq[:], logits[:], over_experts(r_mx[:]), ALU.is_equal))
            step_(dve.tensor_tensor(r_w[:], r_eq[:],
                                    cst[:, C_FIRST].unsqueeze(1).to_broadcast([128, PAIRS, EXPERTS]), ALU.mult))
            step_(dve.tensor_reduce(r_wm[:], r_w[:], AX, ALU.max))
            dve.wait_ge(r_step, done[0])
            dve.tensor_tensor(r_ohb[:], r_w[:], over_experts(r_wm[:]), ALU.is_equal).then_inc(r_counts, 1)
            dve.tensor_copy(vals[:, :, 0], cst[:, C_TOKEN].to_broadcast([128, PAIRS]))
            dve.tensor_copy(vals[:, :, 1], cst[:, C_PAIR])
            dve.wait_ge(r_sb, 1)
            before = s_ps[0][:, 0:PAIRS * EXPERTS].rearrange("p (a e) -> p a e", e=EXPERTS)
            total = s_ps[1][:, 0:PAIRS * EXPERTS].rearrange("p (a e) -> p e a", e=EXPERTS)
            step_(dve.tensor_copy(r_tot[:], total))
            step_(dve.tensor_tensor_scan(r_cum[:].rearrange("p e a -> p (e a)"), one1[:],
                                         r_tot[:].rearrange("p e a -> p (e a)"), 0.0, ALU.mult, ALU.add))
            ends = r_cum[:, :, PAIRS - 1]
            step_(dve.tensor_copy(r_prev[:, 1:EXPERTS], r_cum[:, 0:EXPERTS - 1, PAIRS - 1]))
            step_(dve.scalar_tensor_tensor(out=r_cnt[:], in0=ends, scalar=float(TILE - 1), in1=r_prev[:],
                                           op0=ALU.add, op1=ALU.subtract))
            step_(dve.tensor_scalar(r_nti[:], r_cnt[:], 7, None, ALU.logical_shift_right))
            step_(dve.tensor_copy(r_nt[:], r_nti[:]))
            step_(dve.tensor_tensor_scan(r_end[:], one1[:, 0:EXPERTS], r_nt[:], 0.0, ALU.mult, ALU.add))
            step_(dve.tensor_tensor(r_ends[:], r_end[:].unsqueeze(1).to_broadcast([128, TILES, EXPERTS]),
                                    cst[:, C_IOTA][:, 0:TILES].unsqueeze(2).to_broadcast([128, TILES, EXPERTS]),
                                    ALU.is_le))
            step_(dve.tensor_reduce(r_eidf[:], r_ends[:], AX, ALU.add))
            dve.tensor_scalar(eid[:], r_eidf[:], float(EXPERTS - 1), None, ALU.min).then_inc(eid_done, 1)
            step_(dve.tensor_tensor(r_start[:], r_end[:], r_nt[:], ALU.subtract))
            step_(dve.scalar_tensor_tensor(out=r_base[:], in0=r_start[:], scalar=float(TILE), in1=r_prev[:],
                                           op0=ALU.mult, op1=ALU.subtract))
            step_(dve.tensor_tensor(r_off2[:], r_cum[:], r_base[:].unsqueeze(2).to_broadcast([128, EXPERTS, PAIRS]),
                                    ALU.add))
            step_(dve.tensor_tensor(r_off3[:], before, r_off2[:].rearrange("p e a -> p a e"), ALU.add))
            step_(dve.tensor_tensor(r_pos4[:], r_off3[:], r_ohb[:], ALU.mult))
            step_(dve.tensor_reduce(r_posf[:], r_pos4[:], AX, ALU.add))
            step_(dve.tensor_copy(r_pos[:], r_posf[:]))
            dve.tensor_scalar(r_modi[:], r_pos[:], TILE - 1, None, ALU.bitwise_and)
            step_(dve.tensor_scalar(r_divi[:], r_pos[:], 7, None, ALU.logical_shift_right))
            dve.tensor_copy(r_mod[:], r_modi[:])
            step_(dve.scalar_tensor_tensor(out=r_div[:], in0=r_divi[:], scalar=1.0,
                                           in1=cst[:, C_JUNK].to_broadcast([128, PAIRS]),
                                           op0=ALU.mult, op1=ALU.add))
            dve.tensor_tensor(tile_oh[:], r_div[:].unsqueeze(2).to_broadcast([128, PAIRS, TILES]),
                              iota_b[:, 0:TILES].unsqueeze(1).to_broadcast([128, PAIRS, TILES]), ALU.is_equal)\
                .then_inc(places_done, 1)
            for n in range(0, PAIRS, 8):
                dve.tensor_tensor(slot_oh[:, n:n + 8, :], r_mod[:, n:n + 8].unsqueeze(2).to_broadcast([128, 8, 128]),
                                  iota_b[:].unsqueeze(1).to_broadcast([128, 8, 128]), ALU.is_equal).then_inc(slots_ready, 1)
            dve.wait_ge(index_placed, 1)
            step_(dve.tensor_copy(got[:, INDEX], o_ps[:, 0:2 * TILES].rearrange("p (v t) -> p v t", v=2)))
            dve.tensor_scalar(g_empty[:], got[:, 0], 0.0, float(SKIP), ALU.is_equal, ALU.mult)
            step_(dve.scalar_tensor_tensor(out=g_idx[:], in0=got[:, 1], scalar=float(PAIR_TOKENS), in1=got[:, 0],
                                           op0=ALU.mult, op1=ALU.add))
            dve.tensor_scalar(gather_at[:], g_idx[:], -1.0, 0.0, ALU.add, ALU.max)
            dve.scalar_tensor_tensor(out=scatter_at[:], in0=g_idx[:], scalar=-1.0, in1=g_empty[:],
                                     op0=ALU.add, op1=ALU.add).then_inc(idx_done, 1)
            dve.wait_ge(r_exp, 2)
            step_(dve.tensor_reduce(r_den[:], r_ex[:], AX, ALU.add))
            step_(dve.reciprocal(r_prob[:], r_den[:]))
            step_(dve.tensor_copy(vals[:, :, 2], r_prob[:]))
            step_(dve.tensor_tensor(r_res[:], r_prob[:], vals[:, :, 2], ALU.subtract))
            step_(dve.tensor_copy(vals[:, :, 3], r_res[:]))
            step_(dve.tensor_tensor(r_res2[:], r_res[:], vals[:, :, 3], ALU.subtract))
            step_(dve.tensor_copy(vals[:, :, 4], r_res2[:]))
            tile_values(dve, PROB, prob_ready)
            dve.wait_ge(prob_placed, 1)
            dve.tensor_copy(got[:, PROB], v_ps[:, 0:3 * TILES].rearrange("p (v t) -> p v t", v=3)).then_inc(prob_read, 1)
            dve.wait_ge(prob_read, 1)
            step_(dve.tensor_tensor(g_p12[:], got[:, 2], got[:, 3], ALU.add))
            step_(dve.tensor_tensor(prob[:], g_p12[:], got[:, 4], ALU.add))

            out_ps = (lg_ps, t2_ps)
            dve.wait_ge(w2_in, 16 * (PAIRS + 1))

            def tile_body(tile):
                if t := tile(-1):
                    e = dve.value_load(eid[0:1, bass.ds(t.n, 1)], min_val=0, max_val=EXPERTS - 1)
                    dve.wait_ge(down_mm, t.n + 1)
                    at_least(dve, res_done, t.n)
                    dve.tensor_tensor(yb[:], out_ps[t.par][:, 0:DIM],
                                      b2_sb[:, bass.ds(e, 1), :].rearrange("p e d -> p (e d)"), ALU.add).then_inc(yb_done, 1)
                    dve.wait_ge(yb_done, t.n + 1)
                    at_least(dve, res_out[t.par], t.half * 16)
                    dve.scalar_tensor_tensor(out=res[t.par][:], in0=yb[:], scalar=prob[:, bass.ds(t.n, 1)],
                                             in1=g[t.ring][:, DIM:ROW], op0=ALU.mult, op1=ALU.add).then_inc(res_done, 1)

            tiles_loop(dve, tile_body)


def constants():
    import numpy as np

    c = np.zeros((128, C_WIDTH), np.float32)
    p = np.arange(128)
    c[:, C_IDENT] = np.eye(128)
    c[:, C_IOTA] = p[None, :]
    c[:, C_BEFORE] = np.where((p[:, None] >= p[None, :]) & (p % SLOT < SEQ)[:, None], -1, 0)
    c[:, C_HEADS] = p[:, None] // DH == np.arange(HG)[None, :]
    c[:, C_FIRST] = EXPERTS - np.arange(EXPERTS)[None, :]
    c[:, C_PAIR] = np.arange(PAIRS)[None, :]
    c[:KROWS, C_MEAN] = np.asarray(MULTIPLICITY, np.float64)[:, None] / PATCH_DIM
    c[:, C_VALID] = (p % SLOT < SEQ)[:, None]
    c[:, C_JUNK] = (p % SLOT >= SEQ)[:, None] * 64.0
    c[:, C_TOKEN] = (p // SLOT * SEQ + p % SLOT + 1)[:, None]
    c[:, C_PICK] = (p % 64 == 0)[:, None]
    c[:, C_POWER] = -0.5
    c[:, C_EPS] = LN_EPS
    return c


def lay_out(inputs):
    import numpy as np

    a = {k: np.asarray(v) for k, v in inputs.items()}
    x = a["x"]
    f32 = x.dtype
    padded = np.zeros((IMAGES, CH, SIDE + 2, SIDE + 2), f32)
    padded[:, :, 1:-1, 1:-1] = x
    tokens = np.zeros((KROWS, CHUNKS, BLOCKS * 128), f32)
    for (r, q, c), (chunk, k) in WINDOW.items():
        v = padded[:, c, r + 1:r + 1 + SIDE:PATCH, q + 1:q + 1 + SIDE:PATCH]
        tokens[k, chunk, :TOKENS] = v[:, :GRID, :GRID].reshape(-1)
    xcol = tokens.reshape(KROWS, CHUNKS, BLOCKS, 128).transpose(2, 0, 1, 3)

    moves = ((0, 0), (0, -1), (0, 1), (-1, 0), (1, 0))
    w = a["L0_tok_W"].reshape(PATCH, PATCH, SHIFTS, CH, DIM)
    gb = [a[n].reshape(PATCH, PATCH, SHIFTS, CH) for n in ("L0_tok_ln_gamma", "L0_tok_ln_beta")]
    wtok = np.zeros((KROWS, CHUNKS, SHIFTS, DIM), f32)
    gamma, beta = (np.zeros((KROWS, CHUNKS, SHIFTS), f32) for _ in range(2))
    for (r, q, c), (chunk, k) in WINDOW.items():
        for s, (dr, dq) in enumerate(moves):
            ph, pw = r - dr, q - dq
            if 0 <= ph < PATCH and 0 <= pw < PATCH:
                wtok[k, chunk, s] = w[ph, pw, s, c]
                gamma[k, chunk, s] = gb[0][ph, pw, s, c]
                beta[k, chunk, s] = gb[1][ph, pw, s, c]

    def halves(weight, bias):
        m = np.zeros((HALF + 1, 2, weight.shape[1]), f32)
        m[:HALF] = weight.reshape(2, HALF, -1).transpose(1, 0, 2)
        m[HALF, 0] = bias
        return m

    def qkv_order(m):
        q, k, v = m[..., :DIM], m[..., DIM:2 * DIM], m[..., 2 * DIM:]
        v = v.reshape(v.shape[:-1] + (HG, 2, DH)).swapaxes(-3, -2).reshape(v.shape)
        return np.concatenate([q[..., :HALF], k[..., :HALF], q[..., HALF:], k[..., HALF:], v], axis=-1)

    return {
        "consts": constants(),
        "xcol": xcol,
        "wtok": wtok,
        "gamma": gamma,
        "beta": beta,
        "tok_b": a["L0_tok_b"],
        "wqkv": halves(qkv_order(a["L0_attn_w_attn"]), qkv_order(a["L0_attn_b_attn"])),
        "wproj": halves(a["L0_attn_w_proj"], a["L0_attn_b_proj"]),
        "wrouter": halves(a["L0_ffn_Ws"], a["L0_ffn_bs"]),
        "w1": np.stack([halves(a["L0_ffn_W1"][e], a["L0_ffn_b1"][e]) for e in range(EXPERTS)]),
        "w2": np.ascontiguousarray(a["L0_ffn_W2"].reshape(EXPERTS, FT, 128, DIM).transpose(2, 0, 1, 3)),
        "b2": a["L0_ffn_b2"],
    }


def kernel(**inputs):
    import numpy as np
    import concourse.bacc as bacc
    from concourse.bass_utils import run_bass_kernel_spmd

    nc = bacc.Bacc("TRN2", target_bir_lowering=False, num_devices=1)
    arrays = {k: np.ascontiguousarray(v) for k, v in lay_out(inputs).items()}
    args = [nc.dram_tensor(k, v.shape, mybir.dt.from_np(v.dtype), kind="ExternalInput").ap()
            for k, v in arrays.items()]
    out = nc.dram_tensor("out", (IMAGES, SEQ, DIM), F32, kind="ExternalOutput").ap()
    build(nc, *args, out)
    r = run_bass_kernel_spmd(nc, [arrays], core_ids=[0])
    return r.results[0]["out"]
```

```python
from collections import namedtuple
from contextlib import ExitStack

import concourse.bass as bass
from concourse import mybir
from concourse.alu_op_type import AluOpType as ALU

F32 = mybir.dt.float32
BF16 = mybir.dt.bfloat16
I32 = mybir.dt.int32
U32 = mybir.dt.uint32
ACT = mybir.ActivationFunctionType
AX = mybir.AxisListType.X

IMAGES, CH, SIDE, PATCH = 64, 3, 112, 16
GRID = SIDE // PATCH
SEQ = GRID * GRID
TOKENS = IMAGES * SEQ
DIM = 192
HALF = DIM // 2
HEADS, DH = 12, 16
GROUPS, HG = 2, 6
EXPERTS, FFN = 8, 768
SHIFTS = 5
PATCH_DIM = PATCH * PATCH * SHIFTS * CH
LN_EPS = 1e-5

PAIRS = IMAGES // 2
SLOT = 64
PAIR_TOKENS = 2 * SEQ
SPAN = SEQ + SLOT

BLOCKS = -(-TOKENS // 128)
LAST_ROWS = TOKENS - (BLOCKS - 1) * 128

CHUNKS = 8
MULTIPLICITIES = (5, 4, 3, 1)

TILE = 128
TILES = (TOKENS + EXPERTS * (TILE - 1)) // TILE
FT = FFN // 128
FH = FT // 2
ROW = 2 * DIM
VALUES = 5
INDEX, PROB = slice(0, 2), slice(2, 5)
EARLY = PAIRS - 4
SKIP = 8192

Step = namedtuple("Step", "n half par quad ring")


def window():
    pixels = []
    for r in range(-1, PATCH + 1):
        for q in range(-1, PATCH + 1):
            if 0 <= r < PATCH or 0 <= q < PATCH:
                m = sum(0 <= r + dr < PATCH and 0 <= q + dq < PATCH
                        for dr, dq in ((0, 0), (0, 1), (0, -1), (1, 0), (-1, 0)))
                pixels += [(m, r, q, c) for c in range(CH)]
    place, multiplicity, base = {}, [], 0
    for m in MULTIPLICITIES:
        mine = [x[1:] for x in pixels if x[0] == m]
        for n, x in enumerate(mine):
            place[x] = (n % CHUNKS, base + n // CHUNKS)
        rows = -(-len(mine) // CHUNKS)
        multiplicity += [m] * rows
        base += rows
    return place, multiplicity


WINDOW, MULTIPLICITY = window()
KROWS = len(MULTIPLICITY)
SHIFTED = sum(m > 1 for m in MULTIPLICITY)

_at = 0


def _columns(n):
    global _at
    _at += n
    return slice(_at - n, _at)


C_IDENT = _columns(128)
C_IOTA = _columns(128)
C_BEFORE = _columns(128)
C_HEADS = _columns(HG)
C_FIRST = _columns(EXPERTS)
C_PAIR = _columns(PAIRS)
C_MEAN = _columns(1)
C_VALID = _columns(1)
C_JUNK = _columns(1)
C_TOKEN = _columns(1)
C_PICK = _columns(1)
C_POWER = _columns(1)
C_EPS = _columns(1)
C_WIDTH = _at


def at_least(eng, sem, value):
    if not isinstance(value, int) or value > 0:
        eng.wait_ge(sem, value)


FIRST_BLOCK = Step(0, 0, 0, 0, 0)


def is_first(step):
    return isinstance(step.n, int) and step.n == 0


def fixed_steps(i, count):
    def at(k):
        n = i + k
        return Step(n, n // 2, n % 2, n // 4, n % 4) if 0 <= n < count else None
    return at


def moving_steps(j, u):
    def at(k):
        c = 5 + u + k
        return Step(j * 4 + c, j * 2 + c // 2, c % 2, j + c // 4, c % 4)
    return at


def blocks_loop(eng, body):
    trips = (BLOCKS - 8) // 4
    for i in range(-3, 5):
        body(fixed_steps(i, BLOCKS))
    with eng.Fori(0, trips) as j:
        for u in range(4):
            body(moving_steps(j, u))
    for i in range(5 + 4 * trips, BLOCKS - 1):
        body(fixed_steps(i, BLOCKS))


def pairs_loop(eng, body, block_body, blocks_first=False):
    for i in range(-1, 5):
        steps = [(body, fixed_steps(i, PAIRS))]
        if 0 <= i < 4:
            steps.insert(0 if blocks_first else 1, (block_body, fixed_steps(BLOCKS - 1 + i, BLOCKS)))
        for step, at in steps:
            step(at)
    with eng.Fori(0, (PAIRS - 8) // 4) as j:
        for u in range(4):
            body(moving_steps(j, u))
    for i in range(PAIRS - 3, PAIRS + 3):
        body(fixed_steps(i, PAIRS))


def tiles_loop(eng, body):
    for i in range(-2, 5):
        body(fixed_steps(i, TILES))
    with eng.Fori(0, (TILES - 8) // 4) as j:
        for u in range(4):
            body(moving_steps(j, u))
    for i in range(TILES - 3, TILES + 1):
        body(fixed_steps(i, TILES))


def build(nc, consts, xcol, wtok, gamma_beta, tok_b, wqkv, wproj, wrouter, w1, w2, b2, out):
    assert PAIRS % 4 == 0 and TILES % 4 == 0
    with ExitStack() as ctx:
        def sb(name, shape, dt=F32):
            return ctx.enter_context(nc.sbuf_tensor(name, shape, dt))

        def bank(name):
            return ctx.enter_context(nc.psum_tensor(name, [128, 512], F32))

        def sem(name):
            return ctx.enter_context(nc.semaphore(name))

        h0_dram = nc.dram_tensor("token_h0", [TOKENS, DIM], F32, kind="Internal").ap()
        rows_dram = nc.dram_tensor("token_rows", [TOKENS, ROW], F32, kind="Internal").ap()
        out_rows = out.rearrange("b s d -> (b s) d")

        cst = sb("cst", [128, C_WIDTH])
        ident = cst[:, C_IDENT]
        gb = sb("gb", [KROWS, 2, CHUNKS, SHIFTS])
        gam, bet = gb[:, 0], gb[:, 1]
        tokb = sb("tokb", [1, DIM])
        ones = sb("ones", [128, 128])
        weff = sb("weff", [KROWS, CHUNKS, DIM + 1])
        c1 = sb("c1", [128, DIM])
        c0 = sb("c0", [128, DIM])
        wqkv_sb = sb("wqkv_sb", [HALF + 1, 2, 3 * DIM])
        wproj_sb = sb("wproj_sb", [HALF + 1, 2, DIM])
        wrouter_sb = sb("wrouter_sb", [HALF + 1, 2, EXPERTS])
        w2_sb = sb("w2_sb", [128, EXPERTS, FT, DIM])
        wt_in = w2_sb[0:KROWS].rearrange("k e f d -> k (e f) d")[:, 0:CHUNKS * SHIFTS, :]\
            .rearrange("k (c s) d -> k c s d", c=CHUNKS)
        b2_sb = sb("b2_sb", [128, EXPERTS, DIM])

        x_mem = sb("x_mem", [128, 4, CHUNKS * 128])
        xt = [x_mem[0:KROWS, i].rearrange("k (c t) -> k c t", c=CHUNKS) for i in range(4)]
        sq = [sb(f"sq{i}", [KROWS, CHUNKS, 128]) for i in range(2)]
        sqr = [sb(f"sqr{i}", [KROWS, 128]) for i in range(2)]
        c0_half = sb("c0_half", [128, DIM])
        tok_st = sb("tok_st", [128, 2])
        tok_m2 = sb("tok_m2", [128, 1])
        tok_var = sb("tok_var", [128, 1])
        tok_rs = sb("tok_rs", [128, 1])
        hb = [sb(f"hb{i}", [128, DIM]) for i in range(2)]
        bn1, mv1, ve1, rs1 = (sb(n, [128, k]) for n, k in (("bn1", 6), ("mv1", 2), ("ve1", 1), ("rs1", 1)))
        bn2, mv2, ve2, rs2 = (sb(n, [128, k]) for n, k in (("bn2", 6), ("mv2", 2), ("ve2", 1), ("rs2", 1)))
        xn = [sb(f"xn{i}", [128, DIM]) for i in range(2)]
        xnT = sb("xnT", [HALF, 2, BLOCKS * 128])
        xp = [sb(f"xp{i}", [HALF + 1, 2, SPAN]) for i in range(2)]
        h0 = [sb(f"h0_{i}", [128, DIM]) for i in range(4)]
        qk = [sb(f"qk{i}", [HALF, 2 * GROUPS, SPAN]) for i in range(2)]
        km = sb("km", [HALF, GROUPS, 2, HG, SEQ])
        vb = [sb(f"vb{i}", [128, 2, HG, 2 * DH]) for i in range(4)]
        ss = sb("ss", [128, GROUPS, HG, SEQ])
        smx = sb("smx", [128, GROUPS, HG])
        ex = sb("ex", [128, GROUPS, HG, SEQ])
        pr = sb("pr", [128, HEADS, SLOT])
        prT = sb("prT", [128, HG, 128])
        den = sb("den", [128, GROUPS, HG])
        rden = sb("rden", [128, GROUPS, HG])
        oT = sb("oT", [HALF + 1, 2, 128])
        row = [sb(f"row{i}", [128, ROW]) for i in range(2)]
        x2T = sb("x2T", [HALF + 1, 2, 128])
        logits = sb("logits", [128, PAIRS, EXPERTS])

        qk_ps, v_ps, s0_ps, s1_ps, pt0_ps, pt1_ps, o_ps, t3_ps = (
            bank(n) for n in ("qk_ps", "v_ps", "s0_ps", "s1_ps", "pt0_ps", "pt1_ps", "o_ps", "t3_ps"))
        s_ps, pt_ps = (s0_ps, s1_ps), (pt0_ps, pt1_ps)
        pj_ps = o_ps[:, 256:256 + DIM]
        lg_ps = t3_ps[:, 256:256 + EXPERTS]
        y_ps, t1_ps, c1_ps, c0_ps = (pt0_ps, pt1_ps, v_ps, o_ps), t3_ps, s0_ps, s1_ps

        r_mx = sb("r_mx", [128, PAIRS])
        r_sh = sb("r_sh", [128, PAIRS, EXPERTS])
        r_ex = sb("r_ex", [128, PAIRS, EXPERTS])
        r_den = sb("r_den", [128, PAIRS])
        r_prob = sb("r_prob", [128, PAIRS])
        r_eq = sb("r_eq", [128, PAIRS, EXPERTS])
        r_w = sb("r_w", [128, PAIRS, EXPERTS])
        r_wm = sb("r_wm", [128, PAIRS])
        r_ohb = sb("r_ohb", [128, PAIRS, EXPERTS], BF16)
        before_b = sb("before_b", [128, 128], BF16)
        valid_b = sb("valid_b", [128, 128], BF16)
        iota_b = sb("iota_b", [128, 128], BF16)
        one1 = sb("one1", [128, EXPERTS * PAIRS])
        r_cum = sb("r_cum", [128, EXPERTS, PAIRS])
        r_prev = sb("r_prev", [128, EXPERTS])
        r_cnt = sb("r_cnt", [128, EXPERTS], I32)
        r_nti = sb("r_nti", [128, EXPERTS], I32)
        r_nt = sb("r_nt", [128, EXPERTS])
        r_end = sb("r_end", [128, EXPERTS])
        r_start = sb("r_start", [128, EXPERTS])
        r_base = sb("r_base", [128, EXPERTS])
        r_off = sb("r_off", [128, PAIRS, EXPERTS])
        r_off2 = sb("r_off2", [128, PAIRS, EXPERTS])
        r_pos4 = sb("r_pos4", [128, PAIRS, EXPERTS])
        r_posf = sb("r_posf", [128, PAIRS])
        r_pos = sb("r_pos", [128, PAIRS], I32)
        r_modi = sb("r_modi", [128, PAIRS], I32)
        r_divi = sb("r_divi", [128, PAIRS], I32)
        r_mod = sb("r_mod", [128, PAIRS], BF16)
        r_div = sb("r_div", [128, PAIRS], BF16)
        r_ends = sb("r_ends", [128, TILES, EXPERTS])
        r_eidf = sb("r_eidf", [128, TILES])
        eid = sb("eid", [128, TILES], I32)
        vals = sb("vals", [128, PAIRS, VALUES], BF16)
        r_res = sb("r_res", [128, PAIRS])
        r_res2 = sb("r_res2", [128, PAIRS])
        slot_oh = sb("slot_oh", [128, PAIRS, 128], BF16)
        tile_oh = sb("tile_oh", [128, PAIRS, TILES], BF16)
        tile_v = sb("tile_v", [128, PAIRS, VALUES, TILES], BF16)
        got = sb("got", [128, VALUES, TILES])
        g_idx = sb("g_idx", [128, TILES])
        g_empty = sb("g_empty", [128, TILES])
        g_p12 = sb("g_p12", [128, TILES])
        prob = sb("prob", [128, TILES])
        gather_at = sb("gather_at", [128, TILES], U32)
        scatter_at = sb("scatter_at", [128, TILES], U32)

        w1s = [x_mem[0:HALF + 1, 2 * i:2 * i + 2].rearrange("k a f -> k (a f)")[:, 0:2 * FFN]
               .rearrange("k (a f) -> k a f", a=2) for i in range(2)]
        g = [sb(f"g{i}", [128, ROW]) for i in range(4)]
        gT = sb("gT", [HALF + 1, 2, 128])
        hT = [sb(f"hT{i}", [128, FT, TILE]) for i in range(2)]
        yb = sb("yb", [128, DIM])
        g_at = [sb(f"g_at{i}", [128, 1], U32) for i in range(4)]
        s_at = [sb(f"s_at{i}", [128, 1], U32) for i in range(2)]
        res = [sb(f"res{i}", [128, DIM]) for i in range(2)]

        consts_in, gb_in, wq_in, w2_in = sem("consts_in"), sem("gb_in"), sem("wq_in"), sem("w2_in")
        wt_in_sem = [sem(f"wt_in{c}") for c in range(CHUNKS)]
        h0_zero = sem("h0_zero")
        init_done = sem("init_done")
        weff_first, weff_step = sem("weff_first"), sem("weff_step")
        c1_mm, c1_sb, centred = sem("c1_mm"), sem("c1_sb"), sem("centred")
        c0_half_mm, c0_half_sb, c0_mm, c0_sb = sem("c0_half_mm"), sem("c0_half_sb"), sem("c0_mm"), sem("c0_sb")
        x_in = [sem(f"x_in{i}") for i in range(4)]
        hb_out = [sem(f"hb_out{i}") for i in range(2)]
        h0_in = [sem(f"h0_in{i}") for i in range(4)]
        xp_done = sem("xp_done")
        sq_done, sqr_done, tok_mm = sem("sq_done"), sem("sqr_done"), sem("tok_mm")
        st_done, m2_done, var_done, tok_rstd, hb_done = (
            sem("st_done"), sem("m2_done"), sem("var_done"), sem("tok_rstd"), sem("hb_done"))
        bn1_done, mv1_done, ve1_done, rs1_done, xn_done = (
            sem("bn1_done"), sem("mv1_done"), sem("ve1_done"), sem("rs1_done"), sem("xn_done"))
        t1_mm, xnT_done, qk_mm, v_mm, qk_sb, km_done, v_sb = (
            sem("t1_mm"), sem("xnT_done"), sem("qk_mm"), sem("v_mm"), sem("qk_sb"), sem("km_done"), sem("v_sb"))
        s_mm, smax, ssub, exp_done, den_done, rden_done, p_done, pt_mm, pt_sb = (
            sem("s_mm"), sem("smax"), sem("ssub"), sem("exp_done"), sem("den_done"), sem("rden_done"),
            sem("p_done"), sem("pt_mm"), sem("pt_sb"))
        pv_mm, oT_done, pj_mm = sem("pv_mm"), sem("oT_done"), sem("pj_mm")
        h1_done, bn2_done, mv2_done, ve2_done, rs2_done, xn2_done = (
            sem("h1_done"), sem("bn2_done"), sem("mv2_done"), sem("ve2_done"), sem("rs2_done"), sem("xn2_done"))
        row_out = [sem(f"row_out{i}") for i in range(2)]
        t3_mm, x2T_done, lg_mm, lg_done = sem("t3_mm"), sem("x2T_done"), sem("lg_mm"), sem("lg_done")
        r_step = sem("r_step")
        r_exp, r_counts, r_sb = sem("r_exp"), sem("r_counts"), sem("r_sb")
        places_done, slots_ready = sem("places_done"), sem("slots_ready")
        index_ready, index_placed = sem("index_ready"), sem("index_placed")
        prob_ready, prob_placed, prob_read = sem("prob_ready"), sem("prob_placed"), sem("prob_read")
        eid_done, idx_done = sem("eid_done"), sem("idx_done")
        w1_in = [sem(f"w1_in{i}") for i in range(2)]
        g_in = [sem(f"g_in{i}") for i in range(4)]
        gt_mm, gT_done, up_mm, gelu_done, down_mm = (
            sem("gt_mm"), sem("gT_done"), sem("up_mm"), sem("gelu_done"), sem("down_mm"))
        yb_done, res_done = sem("yb_done"), sem("res_done")
        g_at_done, s_at_done = sem("g_at_done"), sem("s_at_done")
        res_out = [sem(f"res_out{i}") for i in range(2)]

        waited = [sem("waited_dve"), sem("waited_pool")]

        def apart(eng):
            eng.sem_inc(waited[0 if eng is nc.vector else 1], 1)

        def tile_values(eng, values, ready):
            for n in range(0, PAIRS, 8):
                for v in range(values.start, values.stop):
                    ins = eng.tensor_tensor(tile_v[:, n:n + 8, v, :], tile_oh[:, n:n + 8, :],
                                            vals[:, n:n + 8, v].unsqueeze(2).to_broadcast([128, 8, TILES]), ALU.mult)
                ins.then_inc(ready, 1)

        block = ctx.enter_context(nc.Block())

        @block.sync
        def _(sp):
            sp.dma_start(gb[:], gamma_beta).then_inc(gb_in, 16)
            for c in range(CHUNKS):
                sp.dma_start(wt_in[:, c, 0], wtok[:, c, 0]).then_inc(wt_in_sem[c], 16)
                sp.dma_start(wt_in[0:SHIFTED, c, 1:], wtok[0:SHIFTED, c, 1:]).then_inc(wt_in_sem[c], 16)

            def load_x(b):
                at_least(sp, tok_mm, b.n - 3)
                at_least(sp, sq_done, b.n - 3)
                src = xcol[bass.ds(b.n, 1)].rearrange("a k c t -> (a k) c t")
                sp.dma_start(xt[b.ring][:], src).then_inc(x_in[b.ring], 16)

            def store_embedding(b):
                sp.wait_ge(hb_done, b.n + 1)
                rows = LAST_ROWS if isinstance(b.n, int) and b.n == BLOCKS - 1 else 128
                sp.dma_start(h0_dram[bass.ds(b.n * 128, rows), :], hb[b.par][0:rows, :]).then_inc(hb_out[b.par], 16)

            def block_body(block):
                if b := block(3):
                    load_x(b)
                if b := block(-1):
                    store_embedding(b)

            blocks_loop(sp, block_body)

            def load_second_layer(p):
                if isinstance(p.n, int) and p.n == 0:
                    sp.wait_ge(c0_half_mm, 1)
                    sp.wait_ge(centred, CHUNKS)
                    sp.dma_start(b2_sb[:], b2.unsqueeze(0).to_broadcast([128, EXPERTS, DIM])).then_inc(w2_in, 16)
                width = EXPERTS * FT * DIM // PAIRS
                part = bass.ds(p.n * width, width)
                sp.dma_start(w2_sb[:].rearrange("k e f d -> k (e f d)")[:, part],
                             w2.rearrange("k e f d -> k (e f d)")[:, part]).then_inc(w2_in, 16)

            def load_embedding(p):
                if isinstance(p.n, int) and p.n == 0:
                    for i in range(2):
                        sp.wait_ge(hb_out[i], 16 * ((BLOCKS + 1 - i) // 2))
                at_least(sp, h1_done, p.n - 3)
                for a in range(2):
                    sp.dma_start(h0[p.ring][a * SLOT:a * SLOT + SEQ, :],
                                 h0_dram[bass.ds(p.n * PAIR_TOKENS + a * SEQ, SEQ), :]).then_inc(h0_in[p.ring], 16)

            def store_rows(p):
                sp.wait_ge(xn2_done, p.n + 1)
                for a in range(2):
                    sp.dma_start(rows_dram[bass.ds(p.n * PAIR_TOKENS + a * SEQ, SEQ), :],
                                 row[p.par][a * SLOT:a * SLOT + SEQ, :]).then_inc(row_out[p.par], 16)

            def body(pair):
                if p := pair(-1):
                    load_embedding(p)
                if p := pair(0):
                    load_second_layer(p)
                if p := pair(-3):
                    store_rows(p)

            pairs_loop(sp, body, block_body, blocks_first=True)

            sp.wait_ge(eid_done, 1)

            def tile_body(tile):
                if t := tile(2):
                    at_least(sp, up_mm, 2 * (t.n - 1))
                    e = sp.value_load(eid[0:1, bass.ds(t.n, 1)], min_val=0, max_val=EXPERTS - 1)
                    sp.dma_start(w1s[t.par][:], w1[bass.ds(e, 1)].rearrange("e k c f -> (e k) c f"))\
                        .then_inc(w1_in[t.par], 16)

            tiles_loop(sp, tile_body)
            for i in range(2):
                sp.wait_ge(row_out[i], 32 * (PAIRS // 2))
                sp.wait_ge(res_out[i], 16 * (TILES // 2))

        @block.tensor
        def _(pe):
            def sum_beta(first):
                for s in range(SHIFTS):
                    for i in range(2):
                        c = first + i
                        if s == 0:
                            pe.wait_ge(wt_in_sem[c], 32)
                        rows = KROWS if s == 0 else SHIFTED
                        mm = pe.matmul(c0_ps[i * 64:(i + 1) * 64, 0:DIM],
                                       bet[0:rows, c, s:s + 1].to_broadcast([rows, 64]), wt_in[0:rows, c, s, :],
                                       start=(first == 0 and s == 0), stop=(first == CHUNKS - 2 and s == SHIFTS - 1))
                return mm

            pe.wait_ge(init_done, 1)
            pe.wait_ge(gb_in, 16)
            for c in range(CHUNKS):
                if c % 2 == 0 and c < CHUNKS - 2:
                    sum_beta(c)
                pe.wait_ge(weff_step, 2 * (SHIFTS - 1) * (c // 2 + 1) - 1 + c % 2)
                mm = pe.matmul(c1_ps[:, 0:DIM], ones[0:KROWS, :], weff[:, c, 0:DIM],
                               start=(c == 0), stop=(c == CHUNKS - 1))
            mm.then_inc(c1_mm, 1)
            sum_beta(CHUNKS - 2).then_inc(c0_half_mm, 1)

            def fold_beta():
                pe.wait_ge(c0_half_sb, 1)
                pe.wait_ge(consts_in, 32)
                pe.matmul(c0_ps[:, 256:256 + DIM], cst[:, C_PICK].to_broadcast([128, 128]), c0_half[:, :],
                          start=True, stop=False)
                pe.matmul(c0_ps[:, 256:256 + DIM], ones[0:1, :], tokb[:, :], start=False, stop=True).then_inc(c0_mm, 1)

            def tokens(b):
                pe.wait_ge(x_in[b.ring], 16 * (b.quad + 1))
                at_least(pe, hb_done, b.n - 3)
                y = y_ps[b.ring]
                for c in range(CHUNKS):
                    if isinstance(b.n, int) and b.n == 0:
                        pe.wait_ge(centred, c + 1)
                    pe.matmul(y[:, 0:DIM + 1], xt[b.ring][:, c, :], weff[:, c, :],
                              start=(c == 0), stop=(c == CHUNKS - 1))
                pe.wait_ge(sqr_done, b.n + 1)
                pe.matmul(y[:, DIM + 1:DIM + 2], sqr[b.par][:, :], cst[0:KROWS, C_MEAN],
                          start=True, stop=True).then_inc(tok_mm, 1)

            def turn(src, dst, n, ready, done):
                pe.wait_ge(ready, n + 1)
                for k in range(2):
                    mm = pe.transpose(dst[0:HALF, k * 128:(k + 1) * 128],
                                      src[:, k * HALF:(k + 1) * HALF], ident)
                mm.then_inc(done, 1)

            def block_body(block):
                if b := block(0):
                    tokens(b)
                    if isinstance(b.n, int) and b.n == 0:
                        fold_beta()
                if b := block(-3):
                    at_least(pe, xnT_done, b.n)
                    if isinstance(b.n, int) and b.n == BLOCKS - 1:
                        pe.wait_ge(lg_done, 1)
                    turn(xn[b.par], t1_ps, b.n, xn_done, t1_mm)

            blocks_loop(pe, block_body)

            def project_qk(p):
                pe.wait_ge(xp_done, p.n + 1)
                at_least(pe, qk_sb, p.n)
                for m in range(2 * GROUPS):
                    for k in range(2):
                        kr = HALF + 1 - k
                        mm = pe.matmul(qk_ps[0:HALF, m * PAIR_TOKENS:(m + 1) * PAIR_TOKENS],
                                       wqkv_sb[0:kr, k, m * HALF:(m + 1) * HALF], xp[p.par][0:kr, k, 0:PAIR_TOKENS],
                                       start=(k == 0), stop=(k == 1))
                mm.then_inc(qk_mm, 1)

            def project_v(p, a):
                if a == 0:
                    if isinstance(p.n, int) and p.n == 0:
                        pe.wait_ge(hb_done, BLOCKS - 2)
                    at_least(pe, v_sb, p.n)
                for odd in range(2):
                    w = slice(2 * DIM + odd * HALF, 2 * DIM + (odd + 1) * HALF)
                    for k in range(2):
                        kr = HALF + 1 - k
                        mm = pe.matmul(v_ps[odd * SLOT:(odd + 1) * SLOT, a * HALF:(a + 1) * HALF],
                                       xp[p.par][0:kr, k, a * SEQ:a * SEQ + SLOT], wqkv_sb[0:kr, k, w],
                                       start=(k == 0), stop=(k == 1))
                if a == 1:
                    mm.then_inc(v_mm, 1)

            def scores(p):
                pe.wait_ge(km_done, p.n + 1)
                for gr in range(GROUPS):
                    at_least(pe, ssub, 2 * p.n - 1 + gr)
                    for a in range(2):
                        mm = pe.matmul(s_ps[gr][a * SLOT:(a + 1) * SLOT, 0:HG * SEQ],
                                       qk[p.par][:, 2 * gr, a * SEQ:a * SEQ + SLOT],
                                       km[:, gr, a].rearrange("k h t -> k (h t)"), start=True, stop=True)
                    mm.then_inc(s_mm, 1)

            def turn_probs(p):
                for gr in range(GROUPS):
                    pe.wait_ge(p_done, 2 * p.n + 1 + gr)
                    at_least(pe, pt_sb, 2 * p.n - 1 + gr)
                    for i in range(HG // 2):
                        hp = gr * (HG // 2) + i
                        mm = pe.transpose(pt_ps[gr][:, i * 128:(i + 1) * 128],
                                          pr[:, 2 * hp:2 * hp + 2, :].rearrange("p h t -> p (h t)"), ident)
                    mm.then_inc(pt_mm, 1)

            def mix(p):
                pe.wait_ge(v_sb, p.n + 1)
                at_least(pe, h1_done, p.n)
                for hp in range(HG):
                    if hp % (HG // 2) == 0:
                        pe.wait_ge(pt_sb, 2 * p.n + 1 + hp // (HG // 2))
                    row0, half = hp % 3 * 2 * DH, hp // 3
                    for a in range(2):
                        at = half * 128 + a * SLOT
                        mm = pe.matmul(o_ps[row0:row0 + 2 * DH, at:at + SEQ], vb[p.ring][:, a, hp, :],
                                       prT[:, hp, a * SLOT:a * SLOT + SEQ], start=True, stop=True)
                mm.then_inc(pv_mm, 1)

            def project(p):
                pe.wait_ge(oT_done, p.n + 1)
                for k in range(2):
                    kr = HALF + 1 - k
                    mm = pe.matmul(pj_ps, oT[0:kr, k, :], wproj_sb[0:kr, k, :],
                                   start=(k == 0), stop=(k == 1))
                mm.then_inc(pj_mm, 1)

            def router(p):
                pe.wait_ge(x2T_done, p.n + 1)
                for k in range(2):
                    kr = HALF + 1 - k
                    mm = pe.matmul(lg_ps, x2T[0:kr, k, :], wrouter_sb[0:kr, k, :],
                                   start=(k == 0), stop=(k == 1))
                mm.then_inc(lg_mm, 1)

            def body(pair):
                if p := pair(0):
                    if isinstance(p.n, int) and p.n == 0:
                        pe.wait_ge(wq_in, 16 * 3)
                    project_qk(p)
                if p := pair(-1):
                    scores(p)
                if p := pair(-2):
                    if isinstance(p.n, int) and p.n == 0:
                        pe.wait_ge(hb_done, BLOCKS)
                    turn_probs(p)
                if p := pair(0):
                    project_v(p, 0)
                if p := pair(-2):
                    mix(p)
                if p := pair(-3):
                    if isinstance(p.n, int) and p.n < 2:
                        pe.wait_ge(xnT_done, BLOCKS - 1 + p.n)
                    at_least(pe, lg_done, p.n)
                    turn(row[p.par], t3_ps, p.n, xn2_done, t3_mm)
                if p := pair(0):
                    project_v(p, 1)
                if p := pair(-2):
                    project(p)
                if p := pair(-3):
                    router(p)

            pairs_loop(pe, body, block_body)

            pe.wait_ge(r_counts, 2)
            flat = r_ohb[:].rearrange("p a e -> p (a e)")
            pe.matmul(s_ps[0][:, 0:PAIRS * EXPERTS], before_b[:, :], flat, start=True, stop=True)
            pe.matmul(s_ps[1][:, 0:PAIRS * EXPERTS], valid_b[:, :], r_ohb[:].rearrange("p a e -> p e a"), start=True, stop=True)\
                .then_inc(r_sb, 1)

            def place(values, dst, ready, done):
                for n in range(PAIRS):
                    if n % 8 == 0:
                        pe.wait_ge(slots_ready, n // 8 + 1)
                        pe.wait_ge(ready, n // 8 + 1)
                    mm = pe.matmul(dst[:, 0:TILES * (values.stop - values.start)], slot_oh[:, n, :],
                                   tile_v[:, n, values, :].rearrange("p v t -> p (v t)"),
                                   start=(n == 0), stop=(n == PAIRS - 1))
                mm.then_inc(done, 1)

            place(INDEX, o_ps, index_ready, index_placed)

            h_ps = ((s0_ps, s1_ps), (qk_ps, v_ps))
            out_ps = (pt0_ps, pt1_ps)
            pe.wait_ge(w2_in, 16 * (PAIRS + 1))

            def turn_rows(t):
                pe.wait_ge(g_in[t.ring], 16 * (t.quad + 1))
                at_least(pe, gT_done, t.n)
                for k in range(2):
                    mm = pe.transpose(t3_ps[0:HALF, k * 128:(k + 1) * 128],
                                      g[t.ring][:, k * HALF:(k + 1) * HALF], ident)
                mm.then_inc(gt_mm, 1)

            def up(t):
                pe.wait_ge(gT_done, t.n + 1)
                if isinstance(t.n, int) and t.n == 1:
                    pe.wait_ge(prob_read, 1)
                pe.wait_ge(w1_in[t.par], 16 * (t.half + 1))
                for hb in range(2):
                    at_least(pe, gelu_done, 2 * (t.n - 2) + 1 + hb)
                    for i in range(FH):
                        f = hb * FH + i
                        for k in range(2):
                            kr = HALF + 1 - k
                            mm = pe.matmul(h_ps[t.par][hb][:, i * TILE:(i + 1) * TILE],
                                           w1s[t.par][0:kr, k, f * 128:(f + 1) * 128], gT[0:kr, k, :],
                                           start=(k == 0), stop=(k == 1))
                    mm.then_inc(up_mm, 1)

            def down(t):
                e = pe.value_load(eid[0:1, bass.ds(t.n, 1)], min_val=0, max_val=EXPERTS - 1)
                at_least(pe, yb_done, t.n - 1)
                for f in range(FT):
                    if f % FH == 0:
                        pe.wait_ge(gelu_done, 2 * t.n + 1 + f // FH)
                    mm = pe.matmul(out_ps[t.par][:, 0:DIM], hT[t.par][:, f, :],
                                   w2_sb[:, bass.ds(e, 1), f, :].rearrange("p e d -> p (e d)"),
                                   start=(f == 0), stop=(f == FT - 1))
                mm.then_inc(down_mm, 1)

            def tile_body(tile):
                if t := tile(0):
                    up(t)
                    if isinstance(t.n, int) and t.n == 0:
                        place(PROB, v_ps, prob_ready, prob_placed)
                if t := tile(1):
                    turn_rows(t)
                if t := tile(-1):
                    down(t)

            pe.wait_ge(eid_done, 1)
            tiles_loop(pe, tile_body)

        @block.scalar
        def _(act):
            act.dma_start(tokb[:], tok_b.rearrange("(a d) -> a d", a=1)).then_inc(consts_in, 16)
            act.wait_ge(gb_in, 16)
            for c in range(CHUNKS):
                if c == 1:
                    act.dma_start(cst[:], consts).then_inc(consts_in, 16)
                act.wait_ge(wt_in_sem[c], 32)
                act.activation(weff[:, c, 0:DIM], wt_in[:, c, 0, :], ACT.Copy, scale=gam[:, c, 0:1])\
                    .then_inc(weff_first, 1)

            def square(b):
                act.wait_ge(x_in[b.ring], 16 * (b.quad + 1))
                at_least(act, sqr_done, b.n - 1)
                act.activation(sq[b.par][:], xt[b.ring], ACT.Square).then_inc(sq_done, 1)

            square(FIRST_BLOCK)
            act.wait_ge(c0_half_mm, 1)
            act.copy(c0_half[:], c0_ps[:, 0:DIM]).then_inc(c0_half_sb, 1)
            act.dma_start(wqkv_sb[:], wqkv).then_inc(wq_in, 16)
            act.dma_start(wproj_sb[:], wproj).then_inc(wq_in, 16)
            act.dma_start(wrouter_sb[:], wrouter).then_inc(wq_in, 16)

            def copy_block(b):
                act.wait_ge(t1_mm, b.n + 1)
                act.copy(xnT[:, :, bass.ds(b.n * 128, 128)],
                         t1_ps[0:HALF, 0:256].rearrange("k (a t) -> k a t", a=2)).then_inc(xnT_done, 1)

            def copy_pair(p):
                act.wait_ge(xnT_done, min(BLOCKS, (p.n * PAIR_TOKENS + SPAN - 1) // 128 + 1)
                            if isinstance(p.n, int) else BLOCKS)
                at_least(act, v_mm, p.n - 1)
                act.copy(xp[p.par][0:HALF, :, :], xnT[:, :, bass.ds(p.n * PAIR_TOKENS, SPAN)]).then_inc(xp_done, 1)

            def copy_turned(dst, src, ready, used, n, done):
                act.wait_ge(ready, n + 1)
                at_least(act, used, n)
                act.copy(dst[0:HALF, :, :].rearrange("k a t -> k (a t)"), src[0:HALF, 0:256]).then_inc(done, 1)

            def exps(p, gr):
                act.wait_ge(ssub, 2 * p.n + 1 + gr)
                at_least(act, p_done, 2 * p.n - 1 + gr)
                act.activation(ex[:, gr], ss[:, gr], ACT.Exp, scale=float(DH) ** -0.5).then_inc(exp_done, 1)

            def copy_qk(p):
                act.wait_ge(qk_mm, p.n + 1)
                at_least(act, s_mm, 2 * p.n - 2)
                at_least(act, km_done, p.n - 1)
                act.copy(qk[p.par][:, :, 0:PAIR_TOKENS],
                         qk_ps[0:HALF, 0:4 * PAIR_TOKENS].rearrange("k (m t) -> k m t", m=4)).then_inc(qk_sb, 1)

            def copy_probs(p):
                at_least(act, pv_mm, p.n)
                for gr in range(GROUPS):
                    act.wait_ge(pt_mm, 2 * p.n + 1 + gr)
                    act.copy(prT[:, gr * 3:gr * 3 + 3, :].rearrange("p h s -> p (h s)"),
                             pt_ps[gr][:, 0:384]).then_inc(pt_sb, 1)

            def copy_mixed(p):
                act.wait_ge(pv_mm, p.n + 1)
                at_least(act, pj_mm, p.n)

                def tokens_of(x):
                    return x.rearrange("k (h a t) -> k h a t", h=2, a=2)[:, :, :, 0:SEQ]

                act.copy(tokens_of(oT[0:HALF, :, :].rearrange("k h t -> k (h t)")), tokens_of(o_ps[0:HALF, 0:256]))\
                    .then_inc(oT_done, 1)

            act.wait_ge(init_done, 1)

            def block_body(block):
                if (b := block(2)) and not is_first(b):
                    square(b)
                if b := block(-3):
                    copy_block(b)

            blocks_loop(act, block_body)

            def body(pair):
                if p := pair(0):
                    copy_qk(p)
                if p := pair(-2):
                    copy_probs(p)
                if p := pair(-1):
                    exps(p, 0)
                if p := pair(-2):
                    copy_mixed(p)
                if p := pair(-3):
                    copy_turned(x2T, t3_ps, t3_mm, lg_mm, p.n, x2T_done)
                if p := pair(-1):
                    exps(p, 1)
                if p := pair(1):
                    copy_pair(p)

            pairs_loop(act, body, block_body)

            act.wait_ge(r_exp, 2)
            act.activation(r_ex[:], r_sh[:], ACT.Exp).then_inc(r_exp, 1)

            def gelus(t):
                h_ps = ((s0_ps, s1_ps), (qk_ps, v_ps))
                at_least(act, down_mm, t.n - 1)
                for hb in range(2):
                    act.wait_ge(up_mm, 2 * t.n + 1 + hb)
                    act.activation(hT[t.par][:, hb * FH:(hb + 1) * FH, :].rearrange("p f t -> p (f t)"),
                                   h_ps[t.par][hb][:, 0:FH * TILE], ACT.Gelu).then_inc(gelu_done, 1)

            def copy_rows(t):
                act.wait_ge(gt_mm, t.n + 1)
                at_least(act, up_mm, 2 * t.n)
                act.copy(gT[0:HALF, :, :].rearrange("k a t -> k (a t)"), t3_ps[0:HALF, 0:256]).then_inc(gT_done, 1)

            def tile_body(tile):
                if t := tile(0):
                    gelus(t)
                if t := tile(1):
                    copy_rows(t)

            tiles_loop(act, tile_body)

        @block.gpsimd
        def _(pool):
            for x in h0:
                x_zero = pool.memset(x[:], 0.0)
            x_zero.then_inc(h0_zero, 1)
            pool.wait_ge(init_done, 1)
            pool.wait_ge(consts_in, 32)

            def mask_k(p):
                pool.wait_ge(qk_sb, p.n + 1)
                at_least(pool, s_mm, 2 * p.n)
                heads = cst[0:HALF, C_HEADS].unsqueeze(2).to_broadcast([HALF, HG, SEQ])
                for gr in range(GROUPS):
                    for a in range(2):
                        k = qk[p.par][:, 2 * gr + 1, a * SEQ:(a + 1) * SEQ].unsqueeze(1).to_broadcast([HALF, HG, SEQ])
                        last = pool.tensor_tensor(km[:, gr, a], k, heads, ALU.mult)
                last.then_inc(km_done, 1)

            def divide(p):
                for gr in range(GROUPS):
                    pool.wait_ge(rden_done, 2 * p.n + 1 + gr)
                    at_least(pool, pt_mm, 2 * p.n - 1 + gr)
                    pool.tensor_tensor(pr[:, gr * HG:(gr + 1) * HG, 0:SEQ], ex[:, gr],
                                       rden[:, gr].unsqueeze(2).to_broadcast([128, HG, SEQ]), ALU.mult)\
                        .then_inc(p_done, 1)

            def inverse_deviation(mv, ve, rs, n, ready, ve_sem, done):
                pool.wait_ge(ready, n + 1)
                pool.tensor_tensor(ve[:], mv[:, 1:2], cst[:, C_EPS], ALU.add).then_inc(ve_sem, 1)
                pool.wait_ge(ve_sem, n + 1)
                pool.tensor_tensor(rs[:], ve[:], cst[:, C_POWER], ALU.pow).then_inc(done, 1)

            def token_deviation(p):
                pool.wait_ge(st_done, p.n + 1)
                pool.tensor_tensor(tok_m2[:], tok_st[:, 0:1], tok_st[:, 0:1], ALU.mult).then_inc(m2_done, 1)
                pool.wait_ge(m2_done, p.n + 1)
                pool.tensor_tensor(tok_var[:], tok_st[:, 1:2], tok_m2[:], ALU.subtract).then_inc(var_done, 1)
                pool.wait_ge(var_done, p.n + 1)
                pool.tensor_tensor(tok_rs[:], tok_var[:], cst[:, C_POWER], ALU.pow).then_inc(tok_rstd, 1)

            def block_body(block):
                if b := block(-1):
                    token_deviation(b)
                    inverse_deviation(mv1, ve1, rs1, b.n, mv1_done, ve1_done, rs1_done)

            blocks_loop(pool, block_body)

            def body(pair):
                if p := pair(-3):
                    inverse_deviation(mv2, ve2, rs2, p.n, mv2_done, ve2_done, rs2_done)
                if p := pair(0):
                    mask_k(p)
                if p := pair(-1):
                    divide(p)

            pairs_loop(pool, body, block_body)

            pool.wait_ge(places_done, 1)
            tile_values(pool, INDEX, index_ready)

            pool.wait_ge(idx_done, 1)
            for i in range(2):
                pool.wait_ge(row_out[i], 32 * (PAIRS // 2))

            def gather(t):
                at_least(pool, res_done, t.n - 3)
                apart(pool)
                pool.tensor_copy(g_at[t.ring][:], gather_at[:, bass.ds(t.n, 1)]).then_inc(g_at_done, 1)
                pool.wait_ge(g_at_done, t.n + 1)
                apart(pool)
                pool.indirect_dma_start(g[t.ring][:, :], None, rows_dram[:, :],
                                        bass.IndirectOffsetOnAxis(ap=g_at[t.ring][:, 0:1], axis=0))\
                    .then_inc(g_in[t.ring], 16)

            def scatter(t):
                pool.wait_ge(res_done, t.n + 1)
                at_least(pool, res_out[t.par], t.half * 16)
                apart(pool)
                pool.tensor_copy(s_at[t.par][:], scatter_at[:, bass.ds(t.n, 1)]).then_inc(s_at_done, 1)
                pool.wait_ge(s_at_done, t.n + 1)
                apart(pool)
                pool.indirect_dma_start(out_rows, bass.IndirectOffsetOnAxis(ap=s_at[t.par][:, 0:1], axis=0),
                                        res[t.par][:, :], None, bounds_check=TOKENS - 1, oob_is_err=False)\
                    .then_inc(res_out[t.par], 16)

            def tile_body(tile):
                if t := tile(3):
                    gather(t)
                if t := tile(-1):
                    scatter(t)

            gather(Step(0, 0, 0, 0, 0))
            tiles_loop(pool, tile_body)

        @block.vector
        def _(dve):
            dve.memset(ones[:], 1.0)
            dve.memset(one1[:], 1.0)
            dve.memset(oT[0:HALF, :, :], 0.0)
            for x in (*xp, oT, x2T, gT):
                dve.memset(x[HALF:HALF + 1, :, :], 1.0)
            for x in qk:
                dve.memset(x[:, :, PAIR_TOKENS:SPAN], 0.0)
            dve.memset(pr[:, :, SEQ:SLOT], 0.0)
            dve.memset(r_prev[:, 0:1], 0.0)
            for v in vb:
                dve.memset(v[0:SLOT, :, :, DH:2 * DH], 0.0)
                last = dve.memset(v[SLOT:128, :, :, 0:DH], 0.0)
            last.then_inc(init_done, 1)

            dve.wait_ge(gb_in, 16)
            step = 0
            for first in range(0, CHUNKS, 2):
                for s in range(1, SHIFTS):
                    for c in (first, first + 1):
                        if s == 1:
                            dve.wait_ge(weff_first, c + 1)
                        else:
                            dve.wait_ge(weff_step, step - 1)
                        dve.scalar_tensor_tensor(out=weff[0:SHIFTED, c, 0:DIM], in0=wt_in[0:SHIFTED, c, s, :],
                                                 scalar=gam[0:SHIFTED, c, s:s + 1], in1=weff[0:SHIFTED, c, 0:DIM],
                                                 op0=ALU.mult, op1=ALU.add).then_inc(weff_step, 1)
                        step += 1
            dve.wait_ge(consts_in, 32)
            for c in range(CHUNKS):
                dve.tensor_copy(weff[:, c, DIM:DIM + 1], cst[0:KROWS, C_MEAN])

            def sum_squares(b):
                dve.wait_ge(sq_done, b.n + 1)
                at_least(dve, tok_mm, b.n - 1)
                dve.tensor_reduce(sqr[b.par][:, :], sq[b.par][:].rearrange("k c t -> k t c"), AX, ALU.add).then_inc(sqr_done, 1)

            sum_squares(FIRST_BLOCK)
            dve.wait_ge(c1_mm, 1)
            dve.tensor_scalar(c1[:], c1_ps[:, 0:DIM], cst[:, C_MEAN], None, ALU.mult).then_inc(c1_sb, 1)
            dve.wait_ge(c1_sb, 1)
            for c in range(CHUNKS):
                dve.tensor_tensor(weff[:, c, 0:DIM], weff[:, c, 0:DIM], c1[0:KROWS, :], ALU.subtract)\
                    .then_inc(centred, 1)
            def shift_scores(p, gr):
                dve.wait_ge(s_mm, 2 * p.n + 1 + gr)
                v = s_ps[gr][:, 0:HG * SEQ].rearrange("p (h t) -> p h t", h=HG)
                dve.tensor_reduce(smx[:, gr], v, AX, ALU.max).then_inc(smax, 1)
                dve.wait_ge(smax, 2 * p.n + 1 + gr)
                at_least(dve, exp_done, 2 * p.n - 1 + gr)
                dve.tensor_tensor(ss[:, gr], v, smx[:, gr].unsqueeze(2).to_broadcast([128, HG, SEQ]),
                                  ALU.subtract).then_inc(ssub, 1)

            def sum_exps(p, gr):
                dve.wait_ge(exp_done, 2 * p.n + 1 + gr)
                dve.tensor_reduce(den[:, gr], ex[:, gr], AX, ALU.add).then_inc(den_done, 1)
                dve.wait_ge(den_done, 2 * p.n + 1 + gr)
                at_least(dve, p_done, 2 * p.n - 1 + gr)
                dve.reciprocal(rden[:, gr], den[:, gr]).then_inc(rden_done, 1)

            def copy_logits(p):
                dve.wait_ge(lg_mm, p.n + 1)
                dve.tensor_copy(logits[:, bass.ds(p.n, 1), :].rearrange("p a e -> p (a e)"),
                                lg_ps).then_inc(lg_done, 1)

            def copy_v(p):
                dve.wait_ge(v_mm, p.n + 1)
                at_least(dve, pv_mm, p.n - 3)
                v = v_ps[:, 0:DIM].rearrange("p (a h d) -> p a h d", a=2, h=HG)
                dve.tensor_copy(vb[p.ring][0:SLOT, :, :, 0:DH], v[0:SLOT])
                dve.tensor_copy(vb[p.ring][SLOT:128, :, :, DH:2 * DH], v[SLOT:128])\
                    .then_inc(v_sb, 1)

            def statistics(p, src, bn, mv, src_done, bn_sem, mv_sem):
                dve.wait_ge(src_done, p.n + 1)
                dve.bn_stats(bn[:], src).then_inc(bn_sem, 1)
                dve.wait_ge(bn_sem, p.n + 1)
                apart(dve)
                dve.bn_aggr(mv[:], bn[:]).then_inc(mv_sem, 1)

            def add_residual(p):
                dve.wait_ge(pj_mm, p.n + 1)
                dve.wait_ge(h0_in[p.ring], 32 * (p.quad + 1))
                at_least(dve, row_out[p.par], p.half * 32)
                at_least(dve, t3_mm, p.n - 1)
                dve.tensor_tensor(row[p.par][:, DIM:ROW], pj_ps, h0[p.ring][:], ALU.add).then_inc(h1_done, 1)
                statistics(p, row[p.par][:, DIM:ROW], bn2, mv2, h1_done, bn2_done, mv2_done)

            def second_norm(p):
                dve.wait_ge(mv2_done, p.n + 1)
                dve.wait_ge(rs2_done, p.n + 1)
                dve.tensor_scalar(row[p.par][:, 0:DIM], row[p.par][:, DIM:ROW], mv2[:, 0:1], rs2[:, 0:1],
                                  ALU.subtract, ALU.mult).then_inc(xn2_done, 1)

            def token_statistics(b):
                dve.wait_ge(tok_mm, b.n + 1)
                y = y_ps[b.ring]
                dve.tensor_copy(tok_st[:, 0:1], y[:, DIM:DIM + 1])
                dve.tensor_scalar(tok_st[:, 1:2], y[:, DIM + 1:DIM + 2], LN_EPS, None, ALU.add).then_inc(st_done, 1)

            def embed(b):
                if isinstance(b.n, int) and b.n == 0:
                    dve.wait_ge(c0_mm, 1)
                    dve.tensor_copy(c0[:], c0_ps[:, 256:256 + DIM]).then_inc(c0_sb, 1)
                    dve.wait_ge(c0_sb, 1)
                dve.wait_ge(tok_rstd, b.n + 1)
                at_least(dve, hb_out[b.par], b.half * 16)
                dve.scalar_tensor_tensor(out=hb[b.par][:], in0=y_ps[b.ring][:, 0:DIM], scalar=tok_rs[:, 0:1], in1=c0[:],
                                         op0=ALU.mult, op1=ALU.add).then_inc(hb_done, 1)
                statistics(b, hb[b.par][:], bn1, mv1, hb_done, bn1_done, mv1_done)

            def first_norm(b):
                dve.wait_ge(mv1_done, b.n + 1)
                at_least(dve, t1_mm, b.n - 1)
                dve.wait_ge(rs1_done, b.n + 1)
                dve.tensor_scalar(xn[b.par][:], hb[b.par][:], mv1[:, 0:1], rs1[:, 0:1],
                                  ALU.subtract, ALU.mult).then_inc(xn_done, 1)

            def block_body(block):
                if b := block(-1):
                    token_statistics(b)
                if (b := block(1)) and not is_first(b):
                    sum_squares(b)
                if b := block(-2):
                    first_norm(b)
                if b := block(-1):
                    embed(b)

            blocks_loop(dve, block_body)
            dve.tensor_copy(valid_b[:], cst[:, C_VALID].to_broadcast([128, 128]))
            dve.tensor_copy(before_b[:], cst[:, C_BEFORE])
            dve.tensor_copy(iota_b[:], cst[:, C_IOTA])
            dve.wait_ge(h0_zero, 1)

            done = [0]

            def issue(ins):
                done[0] += 1
                ins.then_inc(r_step, 1)

            def need(step):
                dve.wait_ge(r_step, step)

            def step_(ins):
                issue(ins)
                need(done[0])

            def first_choices(n0, n1):
                pairs = slice(n0, n1)

                def over(x):
                    return x.unsqueeze(2).to_broadcast([128, n1 - n0, EXPERTS])

                dve.wait_ge(lg_done, n1)
                step_(dve.tensor_reduce(r_mx[:, pairs], logits[:, pairs], AX, ALU.max))
                dve.tensor_tensor(r_sh[:, pairs], logits[:, pairs], over(r_mx[:, pairs]), ALU.subtract).then_inc(r_exp, 1)
                step_(dve.tensor_tensor(r_eq[:, pairs], logits[:, pairs], over(r_mx[:, pairs]), ALU.is_equal))
                step_(dve.tensor_tensor(r_w[:, pairs], r_eq[:, pairs],
                                        cst[:, C_FIRST].unsqueeze(1).to_broadcast([128, n1 - n0, EXPERTS]), ALU.mult))
                step_(dve.tensor_reduce(r_wm[:, pairs], r_w[:, pairs], AX, ALU.max))
                dve.tensor_tensor(r_ohb[:, pairs], r_w[:, pairs], over(r_wm[:, pairs]), ALU.is_equal).then_inc(r_counts, 1)

            def body(pair):
                if p := pair(-3):
                    add_residual(p)
                if p := pair(-1):
                    shift_scores(p, 0)
                if p := pair(-3):
                    second_norm(p)
                    if isinstance(p.n, int) and p.n == PAIRS - 2:
                        first_choices(0, EARLY)
                if p := pair(-1):
                    shift_scores(p, 1)
                    sum_exps(p, 0)
                if p := pair(0):
                    copy_v(p)
                if p := pair(-1):
                    sum_exps(p, 1)
                if p := pair(-3):
                    copy_logits(p)

            pairs_loop(dve, body, block_body)

            first_choices(EARLY, PAIRS)
            dve.tensor_copy(vals[:, :, 0], cst[:, C_TOKEN].to_broadcast([128, PAIRS]))
            dve.tensor_copy(vals[:, :, 1], cst[:, C_PAIR])
            dve.wait_ge(r_sb, 1)
            before = s_ps[0][:, 0:PAIRS * EXPERTS].rearrange("p (a e) -> p a e", e=EXPERTS)
            step_(dve.tensor_tensor_scan(r_cum[:].rearrange("p e a -> p (e a)"), one1[:],
                                         s_ps[1][:, 0:EXPERTS * PAIRS], 0.0, ALU.mult, ALU.add))
            ends = r_cum[:, :, PAIRS - 1]
            issue(dve.tensor_copy(r_prev[:, 1:EXPERTS], r_cum[:, 0:EXPERTS - 1, PAIRS - 1]))
            issue(dve.tensor_tensor(r_off[:], before, r_cum[:].rearrange("p e a -> p a e"), ALU.add))
            need(done[0] - 1)
            step_(dve.scalar_tensor_tensor(out=r_cnt[:], in0=ends, scalar=float(TILE - 1), in1=r_prev[:],
                                           op0=ALU.add, op1=ALU.subtract))
            step_(dve.tensor_scalar(r_nti[:], r_cnt[:], 7, None, ALU.logical_shift_right))
            step_(dve.tensor_copy(r_nt[:], r_nti[:]))
            step_(dve.tensor_tensor_scan(r_end[:], one1[:, 0:EXPERTS], r_nt[:], 0.0, ALU.mult, ALU.add))
            issue(dve.tensor_tensor(r_start[:], r_end[:], r_nt[:], ALU.subtract))
            issue(dve.tensor_tensor(r_ends[:], r_end[:].unsqueeze(1).to_broadcast([128, TILES, EXPERTS]),
                                    cst[:, C_IOTA][:, 0:TILES].unsqueeze(2).to_broadcast([128, TILES, EXPERTS]),
                                    ALU.is_le))
            need(done[0] - 1)
            issue(dve.scalar_tensor_tensor(out=r_base[:], in0=r_start[:], scalar=float(TILE), in1=r_prev[:],
                                           op0=ALU.mult, op1=ALU.subtract))
            need(done[0] - 1)
            issue(dve.tensor_reduce(r_eidf[:], r_ends[:], AX, ALU.add))
            need(done[0] - 1)
            issue(dve.tensor_tensor(r_off2[:], r_off[:], r_base[:].unsqueeze(1).to_broadcast([128, PAIRS, EXPERTS]),
                                    ALU.add))
            need(done[0] - 1)
            dve.tensor_scalar(eid[:], r_eidf[:], float(EXPERTS - 1), None, ALU.min).then_inc(eid_done, 1)
            need(done[0])
            step_(dve.tensor_tensor(r_pos4[:], r_off2[:], r_ohb[:], ALU.mult))
            step_(dve.tensor_reduce(r_posf[:], r_pos4[:], AX, ALU.add))
            step_(dve.tensor_copy(r_pos[:], r_posf[:]))
            dve.tensor_scalar(r_modi[:], r_pos[:], TILE - 1, None, ALU.bitwise_and)
            step_(dve.tensor_scalar(r_divi[:], r_pos[:], 7, None, ALU.logical_shift_right))
            dve.tensor_copy(r_mod[:], r_modi[:])
            step_(dve.scalar_tensor_tensor(out=r_div[:], in0=r_divi[:], scalar=1.0,
                                           in1=cst[:, C_JUNK].to_broadcast([128, PAIRS]),
                                           op0=ALU.mult, op1=ALU.add))
            dve.tensor_tensor(tile_oh[:], r_div[:].unsqueeze(2).to_broadcast([128, PAIRS, TILES]),
                              iota_b[:, 0:TILES].unsqueeze(1).to_broadcast([128, PAIRS, TILES]), ALU.is_equal)\
                .then_inc(places_done, 1)
            for n in range(0, PAIRS, 8):
                dve.tensor_tensor(slot_oh[:, n:n + 8, :], r_mod[:, n:n + 8].unsqueeze(2).to_broadcast([128, 8, 128]),
                                  iota_b[:].unsqueeze(1).to_broadcast([128, 8, 128]), ALU.is_equal).then_inc(slots_ready, 1)
            dve.wait_ge(index_placed, 1)
            step_(dve.tensor_copy(got[:, INDEX], o_ps[:, 0:2 * TILES].rearrange("p (v t) -> p v t", v=2)))
            dve.tensor_scalar(g_empty[:], got[:, 0], 0.0, float(SKIP), ALU.is_equal, ALU.mult)
            step_(dve.scalar_tensor_tensor(out=g_idx[:], in0=got[:, 1], scalar=float(PAIR_TOKENS), in1=got[:, 0],
                                           op0=ALU.mult, op1=ALU.add))
            dve.tensor_scalar(gather_at[:], g_idx[:], -1.0, 0.0, ALU.add, ALU.max)
            dve.scalar_tensor_tensor(out=scatter_at[:], in0=g_idx[:], scalar=-1.0, in1=g_empty[:],
                                     op0=ALU.add, op1=ALU.add).then_inc(idx_done, 1)
            dve.wait_ge(r_exp, 3)
            step_(dve.tensor_reduce(r_den[:], r_ex[:], AX, ALU.add))
            step_(dve.reciprocal(r_prob[:], r_den[:]))
            step_(dve.tensor_copy(vals[:, :, 2], r_prob[:]))
            step_(dve.tensor_tensor(r_res[:], r_prob[:], vals[:, :, 2], ALU.subtract))
            step_(dve.tensor_copy(vals[:, :, 3], r_res[:]))
            step_(dve.tensor_tensor(r_res2[:], r_res[:], vals[:, :, 3], ALU.subtract))
            step_(dve.tensor_copy(vals[:, :, 4], r_res2[:]))
            tile_values(dve, PROB, prob_ready)
            dve.wait_ge(prob_placed, 1)
            dve.tensor_copy(got[:, PROB], v_ps[:, 0:3 * TILES].rearrange("p (v t) -> p v t", v=3)).then_inc(prob_read, 1)
            dve.wait_ge(prob_read, 1)
            step_(dve.tensor_tensor(g_p12[:], got[:, 2], got[:, 3], ALU.add))
            step_(dve.tensor_tensor(prob[:], g_p12[:], got[:, 4], ALU.add))

            out_ps = (pt0_ps, pt1_ps)
            dve.wait_ge(w2_in, 16 * (PAIRS + 1))

            def tile_body(tile):
                if t := tile(-1):
                    e = dve.value_load(eid[0:1, bass.ds(t.n, 1)], min_val=0, max_val=EXPERTS - 1)
                    dve.wait_ge(down_mm, t.n + 1)
                    at_least(dve, res_done, t.n)
                    dve.tensor_tensor(yb[:], out_ps[t.par][:, 0:DIM],
                                      b2_sb[:, bass.ds(e, 1), :].rearrange("p e d -> p (e d)"), ALU.add).then_inc(yb_done, 1)
                    dve.wait_ge(yb_done, t.n + 1)
                    at_least(dve, res_out[t.par], t.half * 16)
                    dve.scalar_tensor_tensor(out=res[t.par][:], in0=yb[:], scalar=prob[:, bass.ds(t.n, 1)],
                                             in1=g[t.ring][:, DIM:ROW], op0=ALU.mult, op1=ALU.add).then_inc(res_done, 1)

            tiles_loop(dve, tile_body)


def constants():
    import numpy as np

    c = np.zeros((128, C_WIDTH), np.float32)
    p = np.arange(128)
    c[:, C_IDENT] = np.eye(128)
    c[:, C_IOTA] = p[None, :]
    c[:, C_BEFORE] = np.where((p[:, None] >= p[None, :]) & (p % SLOT < SEQ)[:, None], -1, 0)
    c[:, C_HEADS] = p[:, None] // DH == np.arange(HG)[None, :]
    c[:, C_FIRST] = EXPERTS - np.arange(EXPERTS)[None, :]
    c[:, C_PAIR] = np.arange(PAIRS)[None, :]
    c[:KROWS, C_MEAN] = np.asarray(MULTIPLICITY, np.float64)[:, None] / PATCH_DIM
    c[:, C_VALID] = (p % SLOT < SEQ)[:, None]
    c[:, C_JUNK] = (p % SLOT >= SEQ)[:, None] * 64.0
    c[:, C_TOKEN] = (p // SLOT * SEQ + p % SLOT + 1)[:, None]
    c[:, C_PICK] = (p % 64 == 0)[:, None]
    c[:, C_POWER] = -0.5
    c[:, C_EPS] = LN_EPS
    return c


def lay_out(inputs):
    import numpy as np

    a = {k: np.asarray(v) for k, v in inputs.items()}
    x = a["x"]
    f32 = x.dtype
    padded = np.zeros((IMAGES, CH, SIDE + 2, SIDE + 2), f32)
    padded[:, :, 1:-1, 1:-1] = x
    tokens = np.zeros((KROWS, CHUNKS, BLOCKS * 128), f32)
    for (r, q, c), (chunk, k) in WINDOW.items():
        v = padded[:, c, r + 1:r + 1 + SIDE:PATCH, q + 1:q + 1 + SIDE:PATCH]
        tokens[k, chunk, :TOKENS] = v[:, :GRID, :GRID].reshape(-1)
    xcol = tokens.reshape(KROWS, CHUNKS, BLOCKS, 128).transpose(2, 0, 1, 3)

    moves = ((0, 0), (0, -1), (0, 1), (-1, 0), (1, 0))
    w = a["L0_tok_W"].reshape(PATCH, PATCH, SHIFTS, CH, DIM)
    gb = np.stack([a[n].reshape(PATCH, PATCH, SHIFTS, CH) for n in ("L0_tok_ln_gamma", "L0_tok_ln_beta")])
    wtok = np.zeros((KROWS, CHUNKS, SHIFTS, DIM), f32)
    gamma_beta = np.zeros((KROWS, 2, CHUNKS, SHIFTS), f32)
    for (r, q, c), (chunk, k) in WINDOW.items():
        at = 0
        for s, (dr, dq) in enumerate(moves):
            ph, pw = r - dr, q - dq
            if 0 <= ph < PATCH and 0 <= pw < PATCH:
                wtok[k, chunk, at] = w[ph, pw, s, c]
                gamma_beta[k, :, chunk, at] = gb[:, ph, pw, s, c]
                at += 1

    def halves(weight, bias):
        m = np.zeros((HALF + 1, 2, weight.shape[1]), f32)
        m[:HALF] = weight.reshape(2, HALF, -1).transpose(1, 0, 2)
        m[HALF, 0] = bias
        return m

    def qkv_order(m):
        q, k, v = m[..., :DIM], m[..., DIM:2 * DIM], m[..., 2 * DIM:]
        v = v.reshape(v.shape[:-1] + (HG, 2, DH)).swapaxes(-3, -2).reshape(v.shape)
        return np.concatenate([q[..., :HALF], k[..., :HALF], q[..., HALF:], k[..., HALF:], v], axis=-1)

    return {
        "consts": constants(),
        "xcol": xcol,
        "wtok": wtok,
        "gamma_beta": gamma_beta,
        "tok_b": a["L0_tok_b"],
        "wqkv": halves(qkv_order(a["L0_attn_w_attn"]), qkv_order(a["L0_attn_b_attn"])),
        "wproj": halves(a["L0_attn_w_proj"], a["L0_attn_b_proj"]),
        "wrouter": halves(a["L0_ffn_Ws"], a["L0_ffn_bs"]),
        "w1": np.stack([halves(a["L0_ffn_W1"][e], a["L0_ffn_b1"][e]) for e in range(EXPERTS)]),
        "w2": np.ascontiguousarray(a["L0_ffn_W2"].reshape(EXPERTS, FT, 128, DIM).transpose(2, 0, 1, 3)),
        "b2": a["L0_ffn_b2"],
    }


def kernel(**inputs):
    import numpy as np
    import concourse.bacc as bacc
    from concourse.bass_utils import run_bass_kernel_spmd

    nc = bacc.Bacc("TRN2", target_bir_lowering=False, num_devices=1)
    arrays = {k: np.ascontiguousarray(v) for k, v in lay_out(inputs).items()}
    args = [nc.dram_tensor(k, v.shape, mybir.dt.from_np(v.dtype), kind="ExternalInput").ap()
            for k, v in arrays.items()]
    out = nc.dram_tensor("out", (IMAGES, SEQ, DIM), F32, kind="ExternalOutput").ap()
    build(nc, *args, out)
    r = run_bass_kernel_spmd(nc, [arrays], core_ids=[0])
    return r.results[0]["out"]
```
